# Optimizing a Trainium2 kernel written in Bass

```python
import numpy as np
import jax
import jax.numpy as jnp

def _softmax(x, axis=-1):
    return jax.nn.softmax(x, axis=axis)

def _gelu(x):
    return jax.nn.gelu(x, approximate=True)

def _silu(x):
    return jax.nn.silu(x)

def _sigmoid(x):
    return jax.nn.sigmoid(x)

def _layernorm(x, axis=-1, eps=1e-05):
    m = jnp.mean(x, axis=axis, keepdims=True)
    v = jnp.var(x, axis=axis, keepdims=True)
    return (x - m) / jnp.sqrt(v + eps)

def _scatter_add(tgt, idx, src, axis=0):
    return tgt.at[idx].add(src)

def _segment_sum(src, seg, n):
    return jax.ops.segment_sum(src, seg, n)
kernel_name = 'mk_decoder_postln_d1_seqx_r4_ecc4c3'

def setup_inputs(seed: int=0):
    np.random.seed(seed)
    _w = jnp.asarray

    def _rec_inputs():
        import jax
        import jax.numpy as jnp
        _rk = jax.random.key(seed)
        x = -0.0003929 + 0.9999 * jax.random.normal(jax.random.fold_in(_rk, 1), (32, 256, 256), jnp.float32)
        _lenS = 256 - jax.random.randint(jax.random.fold_in(_rk, 7), (32,), 0, max(1, 256 // 4) + 1, jnp.int32)
        _lenS2 = 120 - jax.random.randint(jax.random.fold_in(_rk, 8), (32,), 0, max(1, 120 // 4) + 1, jnp.int32)
        _ctx_1024P = jax.random.normal(jax.random.fold_in(_rk, 11), (32, 16, 256), jnp.float32)
        _ctx_1024c = jax.random.dirichlet(jax.random.fold_in(_rk, 511), 0.3 * jnp.ones((16,), jnp.float32), (32, 120))
        _ctx_1024t = jnp.einsum('bsk,bkd->bsd', _ctx_1024c, _ctx_1024P)
        _ctx_1024t = _ctx_1024t * jax.lax.rsqrt(jnp.mean(jnp.square(_ctx_1024t)) + 1e-12) * 0.953939
        ctx_1024 = 2.81802e-05 + 1.00001 * (_ctx_1024t + 0.3 * jax.random.normal(jax.random.fold_in(_rk, 611), (32, 120, 256), jnp.float32))
        fside_1xSxS2_0 = 0.000675642 + 1.00031 * jax.random.normal(jax.random.fold_in(_rk, 12), (1, 256, 120), jnp.float32)
        return (x, ctx_1024, fside_1xSxS2_0)
    x, ctx_1024, fside_1xSxS2_0 = _rec_inputs()

    def _L0_attn_setup():
        import jax, jax.numpy as jnp
        import numpy as np
        DIM_IN, DIM_K, DIM_V, NH = (256, 256, 256, 16)
        DK, DV = (DIM_K // NH, DIM_V // NH)
        key = jax.random.key(seed)
        kx, kq, kk, kv = jax.random.split(key, 4)
        x = jax.random.normal(kx, (4, 512, DIM_IN), dtype=jnp.float32)
        Wq = jax.random.normal(kq, (DIM_K, DIM_IN), dtype=jnp.float32) / np.sqrt(DIM_IN)
        Wk = jax.random.normal(kk, (DK, DIM_IN), dtype=jnp.float32) / np.sqrt(DIM_IN)
        Wv = jax.random.normal(kv, (DV, DIM_IN), dtype=jnp.float32) / np.sqrt(DIM_IN)
        return {'x': x, 'Wq': Wq, 'Wk': Wk, 'Wv': Wv}
    _L0_attn_all = _L0_attn_setup()
    _L0_attn_in = {k: v for k, v in _L0_attn_all.items() if k in ('Wq', 'Wk', 'Wv')}
    del _L0_attn_all

    def _L0_xattn_setup():
        import jax, jax.numpy as jnp
        import numpy as np
        import math
        D = 256
        B, S = (8, 512)

        def _proj(x, W1, b1, W2, b2):
            h = jnp.einsum('bsd,od->bso', x, W1) + b1
            return jnp.einsum('bsd,od->bso', h, W2) + b2
        key = jax.random.key(seed)
        ks = jax.random.split(key, 8)
        q = jax.random.normal(ks[0], (B, S, D), dtype=jnp.float32)
        k = jax.random.normal(ks[1], (B, S, D), dtype=jnp.float32)
        v1 = jax.random.normal(ks[2], (B, S, D), dtype=jnp.float32)
        mask = jax.random.normal(ks[3], (1, S, S), dtype=jnp.float32)
        lim = 1.0 / math.sqrt(D)
        W1 = jax.random.uniform(ks[4], (D, D), jnp.float32, -lim, lim)
        b1 = jax.random.uniform(ks[5], (D,), jnp.float32, -lim, lim)
        W2 = jax.random.uniform(ks[6], (D, D), jnp.float32, -lim, lim)
        b2 = jax.random.uniform(ks[7], (D,), jnp.float32, -lim, lim)
        return {'q': q, 'k': k, 'v1': v1, 'mask': mask, 'W1': W1, 'b1': b1, 'W2': W2, 'b2': b2}
    _L0_xattn_all = _L0_xattn_setup()
    _L0_xattn_in = {k: v for k, v in _L0_xattn_all.items() if k in ('W1', 'b1', 'W2', 'b2')}
    del _L0_xattn_all

    def _L0_ffn_setup():
        import jax, jax.numpy as jnp
        import numpy as np
        TOP_K = 2
        EPS = 1e-09
        key = jax.random.key(seed)
        ks = jax.random.split(key, 6)
        B, T, D, H, E = (4, 512, 256, 512, 8)
        x = jax.random.normal(ks[0], (B, T, D), dtype=jnp.float32)
        Wg = jax.random.normal(ks[1], (E, D), dtype=jnp.float32) * 0.02
        W1 = jax.random.normal(ks[2], (E, 2 * H, D), dtype=jnp.float32) * 0.02
        b1 = jax.random.normal(ks[3], (E, 2 * H), dtype=jnp.float32) * 0.02
        Wo = jax.random.normal(ks[4], (D, H), dtype=jnp.float32) * 0.02
        bo = jax.random.normal(ks[5], (D,), dtype=jnp.float32) * 0.02
        return {'x': x, 'Wg': Wg, 'W1': W1, 'b1': b1, 'Wo': Wo, 'bo': bo}
    _L0_ffn_all = _L0_ffn_setup()
    _L0_ffn_in = {k: v for k, v in _L0_ffn_all.items() if k in ('Wg', 'W1', 'b1', 'Wo', 'bo')}
    del _L0_ffn_all
    return {'x': x, 'ctx_1024': ctx_1024, 'fside_1xSxS2_0': fside_1xSxS2_0, 'L0_attn_Wq': _L0_attn_in['Wq'], 'L0_attn_Wk': _L0_attn_in['Wk'], 'L0_attn_Wv': _L0_attn_in['Wv'], 'L0_xattn_W1': _L0_xattn_in['W1'], 'L0_xattn_b1': _L0_xattn_in['b1'], 'L0_xattn_W2': _L0_xattn_in['W2'], 'L0_xattn_b2': _L0_xattn_in['b2'], 'L0_ffn_Wg': _L0_ffn_in['Wg'], 'L0_ffn_W1': _L0_ffn_in['W1'], 'L0_ffn_b1': _L0_ffn_in['b1'], 'L0_ffn_Wo': _L0_ffn_in['Wo'], 'L0_ffn_bo': _L0_ffn_in['bo']}

def reference(x, ctx_1024, fside_1xSxS2_0, L0_attn_Wq, L0_attn_Wk, L0_attn_Wv, L0_xattn_W1, L0_xattn_b1, L0_xattn_W2, L0_xattn_b2, L0_ffn_Wg, L0_ffn_W1, L0_ffn_b1, L0_ffn_Wo, L0_ffn_bo):
    import jax
    import jax.numpy as jnp

    def _L0_attn_ref(x, Wq, Wk, Wv):
        import jax, jax.numpy as jnp
        import numpy as np
        DIM_IN, DIM_K, DIM_V, NH = (256, 256, 256, 16)
        DK, DV = (DIM_K // NH, DIM_V // NH)
        B, S, _ = x.shape
        scale = 1.0 / np.sqrt(DK)
        q = (x @ Wq.T).reshape(B, S, NH, DK).transpose(0, 2, 1, 3)
        k = x @ Wk.T
        v = x @ Wv.T
        dist = jnp.einsum('bhqd,bkd->bhqk', q, k) * scale
        dist = jax.nn.softmax(dist, axis=-1)
        att = jnp.einsum('bhqk,bkd->bhqd', dist, v)
        return att.transpose(0, 2, 1, 3).reshape(B, S, DIM_V)

    def _L0_xattn_ref(q, k, v1, mask, W1, b1, W2, b2):
        import jax, jax.numpy as jnp
        import numpy as np
        import math
        D = 256
        B, S = (8, 512)

        def _proj(x, W1, b1, W2, b2):
            h = jnp.einsum('bsd,od->bso', x, W1) + b1
            return jnp.einsum('bsd,od->bso', h, W2) + b2
        qp = _proj(q, W1, b1, W2, b2)
        kp = _proj(k, W1, b1, W2, b2)
        scale = 1.0 / math.sqrt(qp.shape[-1])
        qk = jnp.einsum('bqd,bkd->bqk', qp, kp) * scale
        qk = qk + mask
        attn = jax.nn.softmax(qk, axis=-1)
        return jnp.einsum('bqk,bkd->bqd', attn, v1)

    def _L0_ffn_ref(x, Wg, W1, b1, Wo, bo):
        import jax, jax.numpy as jnp
        import numpy as np
        TOP_K = 2
        EPS = 1e-09
        E = Wg.shape[0]
        gate_logits = jnp.einsum('btd,ed->bte', x, Wg)
        gate_scores = jax.nn.softmax(gate_logits, axis=-1)
        topk_val, topk_idx = jax.lax.top_k(gate_scores, TOP_K)
        topk_val = topk_val / (topk_val.sum(axis=-1, keepdims=True) + EPS)
        comb = (jax.nn.one_hot(topk_idx, E, dtype=x.dtype) * topk_val[..., None]).sum(axis=-2)
        out = jnp.zeros_like(x)
        for e in range(E):
            h = jnp.einsum('btd,hd->bth', x, W1[e]) + b1[e]
            a, b = jnp.split(h, 2, axis=-1)
            g = a * jax.nn.sigmoid(b)
            eo = jnp.einsum('bth,dh->btd', g, Wo) + bo
            out = out + eo * comb[..., e:e + 1]
        return out
    x = _layernorm(x + _L0_attn_ref(x, L0_attn_Wq, L0_attn_Wk, L0_attn_Wv), axis=-1)
    x = _layernorm(x + _L0_xattn_ref(x, ctx_1024, ctx_1024, fside_1xSxS2_0, L0_xattn_W1, L0_xattn_b1, L0_xattn_W2, L0_xattn_b2), axis=-1)
    x = _layernorm(x + _L0_ffn_ref(x, L0_ffn_Wg, L0_ffn_W1, L0_ffn_b1, L0_ffn_Wo, L0_ffn_bo), axis=-1)
    return x

_drawn_inputs = setup_inputs


def setup_inputs(seed=0):
    import zlib

    import numpy as np

    out = dict(_drawn_inputs(seed))
    spreads = {}
    factors = {'L0_xattn_b1': 28.254, 'L0_xattn_b2': 24.952, 'L0_ffn_b1': 8.0, 'L0_ffn_bo': 2.713}
    for name, (base, spread) in spreads.items():
        noise = np.random.default_rng([zlib.crc32(name.encode()), seed]).standard_normal(out[name].shape)
        drawn = base * np.exp(spread * noise) if base else spread * noise
        out[name] = jnp.asarray(drawn.astype(out[name].dtype))
    for name, factor in factors.items():
        out[name] = (out[name] * factor).astype(out[name].dtype)
    return out
```

```python
from contextlib import ExitStack

import numpy as np

import concourse.bass as bass
from concourse import mybir

F32 = mybir.dt.float32
BF16 = mybir.dt.bfloat16
U32 = mybir.dt.uint32
ALU = mybir.AluOpType
ACT = mybir.ActivationFunctionType
AX = mybir.AxisListType

P = 128
EPS = 1e-5
GATE_EPS = 1e-9
QPART = (0, 1, 0, 1, 0, 2)
KROWS = 96
MROWS = 3


class Step:

    def __init__(self, j, r):
        self.j, self.r = j, r

    def back(self, k):
        return Step(self.j, self.r - k)

    @property
    def fixed(self):
        return isinstance(self.j, int)

    @property
    def n(self):
        return 4 * self.j + self.r

    @property
    def half(self):
        return 2 * self.j + self.r // 2

    @property
    def s2(self):
        return self.r % 2

    @property
    def s4(self):
        return self.r % 4


def attention(nc, ctx, io, dram):
    B, S, D = io["x"].shape
    SC = io["context"].shape[1]
    NH = 16
    DK = D // NH
    DC = D // P
    QC = S // P
    E = io["wg_t"].shape[1]
    UNITS = 16
    SELF_SCALE = DK ** -0.5
    CROSS_SCALE = D ** -0.5
    GROUP = 4 * SC
    NGROUP = B // 4
    STRIDE = dram["stride"]

    def sb(name, shape, dt=F32):
        return ctx.enter_context(nc.sbuf_tensor(name, shape, dt))

    def ps(name, shape, dt=F32):
        return ctx.enter_context(nc.psum_tensor(name, shape, dt))

    def sem(name):
        return ctx.enter_context(nc.semaphore(name))

    ident = sb("ident", [P, P])
    ident_b = sb("ident_b", [P, P], BF16)
    neg_half = sb("neg_half", [P, QC])
    eps_c = sb("eps_c", [P, QC])
    one_c = sb("one_c", [P, 1])
    wq = sb("wq", [P, DC, D])
    wk = sb("wk", [P, DC, KROWS])
    wv = sb("wv", [P, DC, DK])
    wg = sb("wg", [P, DC, E])
    mask = sb("mask", [P, QC, SC])
    ones_row = sb("ones_row", [1, P])
    iota_e = sb("iota_e", [P, QC, E])
    w1 = sb("w1", [P, DC, D])
    w2t = sb("w2t", [P, DC, D])
    b1c = sb("b1c", [P, DC])
    b2c = sb("b2c", [P, DC])
    wc = sb("wc", [P, DC, D])
    cvec = sb("cvec", [P, DC])
    gram = sb("gram", [P, DC, D])
    uvec = sb("uvec", [P, DC])
    cc = sb("cc", [1, 1])
    ctx_t = sb("ctx_t", [P, DC, 2, GROUP])
    keymap = sb("keymap", [P, DC, B * SC])
    keybias = sb("keybias", [1, B * SC])

    xt = sb("xt", [P, 2, DC, S])
    qpart = sb("qpart", [P, 2, 3, DC, S], BF16)
    qrest = sb("qrest", [P, 2, DC, S])
    krest = sb("krest", [P, 2, S])
    ksmall = sb("ksmall", [P, 2, S], BF16)
    qstack = sb("qstack", [P, 4, NH, S], BF16)
    kstack = sb("kstack", [P, 4, S], BF16)
    vaug = sb("vaug", [P, 4, QC, 32])
    negmax = sb("negmax", [P, 2, NH, QC])
    mrest = sb("mrest", [P, 2, NH, QC])
    mpart = sb("mpart", [P, 2, MROWS, NH, QC], BF16)
    mrows = sb("mrows", [MROWS * NH * QC, 2, P], BF16)
    PT = 8
    probs = sb("probs", [P, PT, 2 * S])
    att_t = sb("att_t", [P, 2, 2 * S])
    rden = sb("rden", [P, 2, QC * 8])
    att = sb("att", [P, 2, QC, D])
    xres = sb("xres", [P, 2, QC, D])
    y1 = sb("y1", [P, 2, QC, D])
    stats1 = sb("stats1", [P, 2, QC, 6])
    mv1 = sb("mv1", [P, 2, QC, 2])
    vare1 = sb("vare1", [P, 2, QC])
    rstd1 = sb("rstd1", [P, 2, QC])
    x1 = sb("x1", [P, 2, QC, D])
    x1t = sb("x1t", [P, 2, DC, S])
    cscore = sb("cscore", [P, 2, QC, SC])
    cnegmax = sb("cnegmax", [P, 2, QC])
    cprob = sb("cprob", [P, 2, QC, SC])
    csum = sb("csum", [P, 2, QC])
    crec = sb("crec", [P, 2, QC])
    cprob_t = sb("cprob_t", [SC, 2, S])
    ctxv = sb("ctxv", [SC, 2, D])
    y2 = sb("y2", [P, 2, QC, D])
    stats2 = sb("stats2", [P, 2, QC, 6])
    mv2 = sb("mv2", [P, 2, QC, 2])
    vare2 = sb("vare2", [P, 2, QC])
    rstd2 = sb("rstd2", [P, 2, QC])
    ROW = D + E + 1
    x2 = sb("x2", [P, 2, QC, ROW])
    x2t = sb("x2t", [P, 2, DC, S])
    logits = sb("logits", [P, 2, QC, E])
    top = sb("top", [P, 2, QC, 8])
    topi = sb("topi", [P, 2, QC, 8], U32)
    topf = sb("topf", [P, 2, QC, 2])
    gneg = sb("gneg", [P, 2, QC])
    gexp = sb("gexp", [P, 2, QC, E])
    gsum = sb("gsum", [P, 2, QC])
    gtop = sb("gtop", [P, 2, QC, 2])
    gden = sb("gden", [P, 2, QC])
    hot = sb("hot", [P, 2, QC, 2, E])
    hotsum = sb("hotsum", [P, 2, QC, E], BF16)
    before = sb("before", [P, P], BF16)
    all_ones = sb("all_ones", [P, P], BF16)
    place = sb("place", [P, 2, QC, E])
    chosen = sb("chosen", [P, 2, QC, 2, E])
    slotf = sb("slotf", [P, 2, QC, 2])
    slots = sb("slots", [P, 2, QC * 2], U32)
    base = dram["base"]

    psS = ps("psS", [P, 2, 512])
    psT = ps("psT", [P, 2, 512])
    psO = ps("psO", [P, 2, 512])
    psA = ps("psA", [P, 512])
    psB = ps("psB", [P, 512])

    names = [
        "setup_loaded", "ctx_group_even", "ctx_group_odd", "consts_made", "wc_product", "c_product", "wc_copied", "gram_product",
        "gram_copied", "keymap_product", "keymap_copied",
        "xt_loaded0", "xt_loaded1", "xres_loaded0", "xres_loaded1", "ctxv_loaded0", "ctxv_loaded1",
        "q_stored", "q_stacked0", "q_stacked1", "m_stacked0", "m_stacked1", "x2_stored0", "x2_stored1",
        "dispatched0", "dispatched1",
        "q_projected", "kv_projected", "max_scored", "m_transposed", "scored", "pv_done", "att_transposed",
        "x1_transposed", "cross_scored", "cprob_transposed", "cross_out", "x2_transposed", "gate_scored", "counted",
        "q1_cast", "kv_cast", "k_mid", "m_copied", "exp_done", "att_copied", "x1t_copied", "cross_exp",
        "cprobt_copied", "x2t_copied", "gate_exp",
        "q_rest", "k_rest", "k_split", "max_reduced", "m_split", "att_normed", "var1_ready", "x1_ready",
        "cross_masked", "y2_ready", "var2_ready", "x2_ready", "gate_max", "hot_ready", "comb_ready", "slots_ready", "slot_link", "stats1_ready",
        "stats2_ready", "den_ready", "m_link", "gate_link", "score_link", "crec_ready",
        "q_split", "y1_ready", "rstd1_ready", "rstd2_ready", "pool_chain",
    ]
    sm = {n: sem(n) for n in names}

    def wait(eng, name, value):
        if isinstance(value, int) and value <= 0:
            return
        eng.wait_ge(sm[name], value)

    def done(b, per=1, k=None):
        k = per if k is None else k
        return per * b.n + k

    def active(b):
        return not b.fixed or 0 <= b.n < B

    def clamp(b):
        return Step(0, B - 1) if b.fixed and b.n >= B else b

    def pipeline(eng, step):
        for r in range(8):
            step(Step(0, r - 1))
        with eng.Fori(2, B // 4) as j:
            for r in range(4):
                step(Step(j, r - 1))
        for r in range(7):
            step(Step(B // 4, r - 1))

    block = ctx.enter_context(nc.Block())

    @block.sync
    def _(sp):
        for dst, src in (
            (wq, io["wq_t"].rearrange("(c p) o -> p c o", p=P)), (wv, io["wv_t"].rearrange("(c p) o -> p c o", p=P)),
            (w1, io["w1"].rearrange("(c p) o -> p c o", p=P)), (w2t, io["w2_t"].rearrange("(c p) o -> p c o", p=P)),
            (wg, io["wg_t"].rearrange("(c p) o -> p c o", p=P)), (mask, io["mask"].rearrange("(c p) k -> p c k", p=P)),
        ):
            sp.dma_start(dst[:, :, :], src).then_inc(sm["setup_loaded"], 16)
        for dst, src in ((b1c, io["b1"]), (b2c, io["b2"])):
            sp.dma_start(dst[:, :], src).then_inc(sm["setup_loaded"], 16)
        for k in range(KROWS // DK):
            sp.dma_start(wk[:, :, k * DK:(k + 1) * DK],
                         io["wk_t"].rearrange("(c p) o -> p c o", p=P)).then_inc(sm["setup_loaded"], 16)
        for g in range(NGROUP):
            if g >= 2:
                sp.wait_ge(sm["keymap_product"], g - 1)
            name = "ctx_group_odd" if g % 2 else "ctx_group_even"
            sp.dma_start(ctx_t[:, :, g % 2, :],
                         io["context_t"][:, g * GROUP:(g + 1) * GROUP].rearrange("(c p) k -> p c k", p=P)
                         ).then_inc(sm[name], 16)

        def load_xt(b):
            if active(b):
                wait(sp, "kv_projected", done(b.back(2)))
                sp.dma_start(xt[:, b.s2], io["x_t"][bass.ds(b.n, 1)].rearrange("o (c p) s -> p (o c) s", p=P)
                             ).then_inc(sm[f"xt_loaded{b.s2}"], 16)

        def step(t):
            load_xt(t.back(-1))
            b = t.back(5)
            if active(b):
                wait(sp, "x2_ready", done(b))
                sp.dma_start(dram["sum"][0:B * S, :].rearrange("(b s) d -> b s d", s=S)[bass.ds(b.n, 1)].rearrange("o (c p) d -> p (o c) d", p=P), x2[:, b.s2, :, 0:D]
                             ).then_inc(sm[f"x2_stored{b.s2}"], 16)
            b = t.back(3)
            if active(b):
                wait(sp, "y1_ready", done(b.back(2)))
                sp.dma_start(xres[:, b.s2], io["x"][bass.ds(b.n, 1)].rearrange("o (c p) d -> p (o c) d", p=P)
                             ).then_inc(sm[f"xres_loaded{b.s2}"], 16)
                wait(sp, "cross_out", done(b.back(2)))
                sp.dma_start(ctxv[:, b.s2], io["context"][bass.ds(b.n, 1)].rearrange("o k d -> (o k) d")
                             ).then_inc(sm[f"ctxv_loaded{b.s2}"], 16)
            b = t.back(2)
            if active(b):
                wait(sp, "m_copied", done(b))
                sp.dma_start(qstack[KROWS:KROWS + MROWS, b.s4], mrows[:, b.s2]).then_inc(sm[f"m_stacked{b.s2}"], 16)
            b = t
            if active(b):
                wait(sp, "q1_cast", done(b))
                wait(sp, "q_split", done(b, 2))
                sp.dma_start(dram["q"][b.s2].rearrange("t (c p) s -> p t c s", p=P), qpart[:, b.s2]
                             ).then_inc(sm["q_stored"], 16)
                wait(sp, "q_stored", done(b, 16))
                wait(sp, "scored", done(b.back(4), UNITS))
                for i, part in enumerate(QPART):
                    sp.dma_start(qstack[i * DK:(i + 1) * DK, b.s4],
                                 dram["q"][b.s2, part].rearrange("(h d) s -> d h s", d=DK)
                                 ).then_inc(sm[f"q_stacked{b.s2}"], 16)

        pipeline(sp, step)
        for s in range(2):
            sp.wait_ge(sm[f"x2_stored{s}"], 16 * (B // 2))

    @block.gpsimd
    def _(pool):
        pool.memset(ident[:, :], 0.0).then_inc(sm["pool_chain"], 1)
        pool.memset(neg_half[:, :], -0.5)
        pool.memset(eps_c[:, :], EPS)
        pool.memset(all_ones[:, :], 1.0)
        pool.memset(before[:, :], 1.0)
        pool.iota(base[:, 0, :], pattern=[[STRIDE, E]], base=0, channel_multiplier=0,
                  allow_small_or_imprecise_dtypes=True)
        for s in range(2):
            pool.iota(x2[:, s, :, D + E], pattern=[[P, QC]], base=s * S, channel_multiplier=1,
                      allow_small_or_imprecise_dtypes=True)
        pool.memset(one_c[:, :], 1.0)
        pool.memset(ones_row[:, :], 1.0)
        pool.iota(iota_e[:, :, :], pattern=[[0, QC], [1, E]], base=0, channel_multiplier=0,
                  allow_small_or_imprecise_dtypes=True)
        pool.memset(vaug[:, :, :, :], 0.0).then_inc(sm["pool_chain"], 1)
        pool.wait_ge(sm["pool_chain"], 2)
        pool.memset(vaug[:, :, :, DK:DK + 1], 1.0)
        pool.affine_select(out=ident[:, :], in_=ident[:, :], compare_op=ALU.not_equal, fill=1.0, base=0,
                           pattern=[[-1, P]], channel_multiplier=1).then_inc(sm["pool_chain"], 1)
        pool.wait_ge(sm["pool_chain"], 3)
        pool.affine_select(out=before[:, :], in_=before[:, :], compare_op=ALU.is_gt, fill=0.0, base=0,
                           pattern=[[1, P]], channel_multiplier=-1)
        pool.tensor_copy(ident_b[:, :], ident[:, :]).then_inc(sm["consts_made"], 1)

        def rstd(b, var, mv, vare, out, ready):
            wait(pool, var, done(b))
            pool.tensor_tensor(vare[:, b.s2], mv[:, b.s2, :, 1], eps_c[:, :], ALU.add).then_inc(sm[ready], 1)
            wait(pool, ready, 2 * b.n + 1)
            pool.tensor_tensor(out[:, b.s2], vare[:, b.s2], neg_half[:, :], ALU.pow).then_inc(sm[ready], 1)

        def step(t):
            b = t.back(5)
            if active(b):
                rstd(b, "var2_ready", mv2, vare2, rstd2, "rstd2_ready")
            b = t
            if active(b):
                wait(pool, "q_rest", done(b))
                wait(pool, "q_stored", done(b.back(2), 16))
                pool.tensor_tensor(qpart[:, b.s2, 1], qrest[:, b.s2], one_c[:, :].unsqueeze(2).to_broadcast([P, DC, S]),
                                   ALU.mult).then_inc(sm["q_split"], 1)
                wait(pool, "q_split", 2 * b.n + 1)
                pool.tensor_tensor(qpart[:, b.s2, 2], qrest[:, b.s2], qpart[:, b.s2, 1], ALU.subtract
                                   ).then_inc(sm["q_split"], 1)
            b = t.back(4)
            if active(b):
                wait(pool, "att_normed", done(b, 2))
                wait(pool, f"xres_loaded{b.s2}", 16 * b.half + 16)
                pool.tensor_tensor(y1[:, b.s2], att[:, b.s2], xres[:, b.s2], ALU.add).then_inc(sm["y1_ready"], 1)
                wait(pool, "slots_ready", done(t.back(6)))
                rstd(b, "var1_ready", mv1, vare1, rstd1, "rstd1_ready")
            b = t.back(6)
            if active(b):
                if b.fixed:
                    wait(pool, "slots_ready", done(b))
                for c in range(QC):
                    for k in range(2):
                        pool.indirect_dma_start(
                            out=dram["lists"], out_offset=bass.IndirectOffsetOnAxis(
                                ap=slots[:, b.s2, 2 * c + k:2 * c + k + 1], axis=0),
                            in_=x2[:, b.s2, c, :], in_offset=None).then_inc(sm[f"dispatched{b.s2}"], 16)

        pipeline(pool, step)
        for s in range(2):
            pool.wait_ge(sm[f"dispatched{s}"], 2 * QC * 16 * (B // 2))

    @block.tensor
    def _(pe):
        mm = nc.tensor.matmul
        pe.wait_ge(sm["setup_loaded"], 16 * (8 + KROWS // DK))
        for oc in range(DC):
            for k in range(DC):
                last = mm(psS[:, oc, 0:D], w2t[:, k, oc * P:(oc + 1) * P], w1[:, k, :], start=k == 0, stop=k == DC - 1)
        last.then_inc(sm["wc_product"], 1)
        for oc in range(DC):
            for k in range(DC):
                last = mm(psT[:, 0, oc:oc + 1], w2t[:, k, oc * P:(oc + 1) * P], b1c[:, k:k + 1], start=k == 0,
                          stop=k == DC - 1)
        last.then_inc(sm["c_product"], 1)
        pe.wait_ge(sm["wc_copied"], 2)
        for ic in range(DC):
            for k in range(DC):
                mm(psS[:, ic, 0:D], wc[:, k, ic * P:(ic + 1) * P], wc[:, k, :], start=k == 0, stop=k == DC - 1)
        for ic in range(DC):
            for k in range(DC):
                mm(psT[:, 1, ic:ic + 1], wc[:, k, ic * P:(ic + 1) * P], cvec[:, k:k + 1], start=k == 0,
                   stop=k == DC - 1)
        for k in range(DC):
            last = mm(psO[0:1, 0, 0:1], cvec[:, k:k + 1], cvec[:, k:k + 1], start=k == 0, stop=k == DC - 1)
        last.then_inc(sm["gram_product"], 1)
        pe.wait_ge(sm["gram_copied"], 2)
        for g in range(NGROUP):
            pe.wait_ge(sm["ctx_group_odd" if g % 2 else "ctx_group_even"], 16 * (g // 2 + 1))
            if g >= 1:
                pe.wait_ge(sm["keymap_copied"], 3 * g)
            for ic in range(DC):
                for k in range(DC):
                    mm(psS[:, ic, 0:GROUP], gram[:, k, ic * P:(ic + 1) * P], ctx_t[:, k, g % 2, :],
                       start=k == 0, stop=k == DC - 1)
            for k in range(DC):
                last = mm(psT[0:1, 0, 0:GROUP], uvec[:, k:k + 1], ctx_t[:, k, g % 2, :], start=k == 0,
                          stop=k == DC - 1)
            last.then_inc(sm["keymap_product"], 1)
        pe.wait_ge(sm["keymap_copied"], 3 * NGROUP)
        pe.wait_ge(sm["consts_made"], 1)

        def att_transpose(b, g):
            wait(pe, "att_copied", 2 * b.n + g + 1)
            if g == 0:
                wait(pe, "y2_ready", done(b.back(1)))
                if b.fixed:
                    wait(pe, "m_copied", done(clamp(b.back(-1))))
            else:
                wait(pe, "att_normed", 2 * b.n + 1)
            for c in range(QC):
                for hh in range(2):
                    last = nc.tensor.transpose(psA[:, (c * 2 + hh) * P:(c * 2 + hh + 1) * P],
                                               att_t[:, g, hh * S + c * P:hh * S + (c + 1) * P], ident[:, :])
            last.then_inc(sm["att_transposed"], 1)

        def step(t):
            b = t.back(4)
            if active(b):
                att_transpose(b, 0)
            b = t
            if active(b):
                wait(pe, f"xt_loaded{b.s2}", 16 * b.half + 16)
                wait(pe, "cprobt_copied", done(b.back(5)))
                wait(pe, "slots_ready", done(b.back(6)))
                if b.fixed:
                    wait(pe, "k_rest", done(b.back(1)))
                    wait(pe, "gate_exp", done(b.back(6)))
                for oc in range(DC):
                    for k in range(DC):
                        last = mm(psB[:, oc * S:(oc + 1) * S], wq[:, k, oc * P:(oc + 1) * P], xt[:, b.s2, k, :],
                                  start=k == 0, stop=k == DC - 1)
                last.then_inc(sm["q_projected"], 1)
            b3, b1 = t.back(3), t.back(1)

            def pv(w):
                g, kc = w // 2, w % 2
                wait(pe, "exp_done", UNITS * b3.n + 4 * w + 4)
                if kc == 0:
                    wait(pe, "att_copied", 2 * b3.n + g - 1)
                for i in range(4):
                    last = mm(psO[32 * i:32 * i + 32, g, :], vaug[:, b3.s4, kc, :], probs[:, (4 * w + i) % PT, :],
                              start=kc == 0, stop=kc == 1)
                last.then_inc(sm["pv_done"], 1)

            for u in range(UNITS):
                if u == 0 and active(t.back(4)):
                    att_transpose(t.back(4), 1)
                if u == 1 and active(t):
                    b = t
                    wait(pe, "q_rest", done(b))
                    for k in range(DC):
                        mm(psB[0:KROWS, 0:S], wk[:, k, :], xt[:, b.s2, k, :], start=k == 0, stop=k == DC - 1)
                    for c in range(QC):
                        for k in range(DC):
                            last = mm(psB[:, S + c * DK:S + (c + 1) * DK], xt[:, b.s2, k, c * P:(c + 1) * P],
                                      wv[:, k, :], start=k == 0, stop=k == DC - 1)
                    last.then_inc(sm["kv_projected"], 1)
                if u == 2 and active(t.back(2)):
                    b = t.back(2)
                    wait(pe, "m_split", done(b))
                    wait(pe, "att_normed", 2 * b.n - 2)
                    if b.fixed:
                        wait(pe, "m_copied", done(b.back(1)))
                        wait(pe, "y2_ready", done(b.back(3)))
                    nc.tensor.transpose(psA[0:MROWS * NH * QC, 0:P // 2].bitcast(BF16),
                                        mpart[:, b.s2].rearrange("p m h c -> p (m h c)"), ident_b[:, :]
                                        ).then_inc(sm["m_transposed"], 1)
                if u == 4 and active(t.back(5)):
                    b = t.back(5)
                    wait(pe, "x2_ready", done(b))
                    wait(pe, "k_rest", done(clamp(t)))
                    if b.fixed:
                        wait(pe, "cprobt_copied", done(b))
                    for c in range(QC):
                        for k in range(DC):
                            last = nc.tensor.transpose(psB[:, k * S + c * P:k * S + (c + 1) * P],
                                                       x2[:, b.s2, c, k * P:(k + 1) * P], ident[:, :])
                    last.then_inc(sm["x2_transposed"], 1)
                if u == 6 and active(t.back(4)):
                    b = t.back(4)
                    wait(pe, "x1_ready", done(b))
                    wait(pe, "m_copied", done(clamp(t.back(2))))
                    for c in range(QC):
                        for k in range(DC):
                            last = nc.tensor.transpose(psA[:, k * S + c * P:k * S + (c + 1) * P],
                                                       x1[:, b.s2, c, k * P:(k + 1) * P], ident[:, :])
                    last.then_inc(sm["x1_transposed"], 1)
                if u == 7 and active(t.back(5)):
                    b = t.back(5)
                    wait(pe, "x2t_copied", done(b))
                    for c in range(QC):
                        for k in range(DC):
                            last = mm(psB[:, c * E:(c + 1) * E], x2t[:, b.s2, k, c * P:(c + 1) * P], wg[:, k, :],
                                      start=k == 0, stop=k == DC - 1)
                    last.then_inc(sm["gate_scored"], 1)
                if u == 8 and active(t.back(4)):
                    b = t.back(4)
                    wait(pe, "x1t_copied", done(b))
                    for c in range(QC):
                        for k in range(DC):
                            mm(psA[:, c * SC:(c + 1) * SC], x1t[:, b.s2, k, c * P:(c + 1) * P],
                               keymap[:, k, bass.ds(b.n * SC, SC)], start=k == 0, stop=False)
                        last = mm(psA[:, c * SC:(c + 1) * SC], ones_row[:, :], keybias[:, bass.ds(b.n * SC, SC)],
                                  start=False, stop=True)
                    last.then_inc(sm["cross_scored"], 1)
                if u == 12 and active(t.back(4)):
                    b = t.back(4)
                    wait(pe, "cross_exp", done(b))
                    wait(pe, "gate_max", done(t.back(5)))
                    for c in range(QC):
                        last = nc.tensor.transpose(psB[0:SC, c * P:(c + 1) * P], cprob[:, b.s2, c, :], ident[:, :])
                    last.then_inc(sm["cprob_transposed"], 1)
                if u == 15 and active(t.back(5)):
                    b = t.back(5)
                    wait(pe, "hot_ready", done(b))
                    wait(pe, "cprobt_copied", done(clamp(t.back(4))))
                    h0, h1 = hotsum[:, b.s2, 0, :], hotsum[:, b.s2, 1, :]
                    mm(psB[:, 0:E], before[:, :], h0, start=True, stop=True)
                    mm(psB[:, E:2 * E], before[:, :], h1, start=True, stop=False)
                    mm(psB[:, E:2 * E], all_ones[:, :], h0, start=False, stop=True)
                    mm(psB[:, 2 * E:3 * E], all_ones[:, :], h0, start=True, stop=False)
                    mm(psB[:, 2 * E:3 * E], all_ones[:, :], h1, start=False, stop=True
                       ).then_inc(sm["counted"], 1)
                if u == 15 and active(t.back(4)):
                    b = t.back(4)
                    wait(pe, "cprobt_copied", done(b))
                    wait(pe, f"ctxv_loaded{b.s2}", 16 * b.half + 16)
                    for c in range(QC):
                        last = mm(psA[:, c * D:(c + 1) * D], cprob_t[:, b.s2, c * P:(c + 1) * P], ctxv[:, b.s2, :],
                                  start=True, stop=True)
                    last.then_inc(sm["cross_out"], 1)
                if active(b1):
                    if u == 0:
                        wait(pe, f"q_stacked{b1.s2}", 6 * 16 * (b1.half + 1))
                        wait(pe, "k_split", done(b1))
                    wait(pe, "max_reduced", UNITS * b1.n + u - 1)
                    c, hp = u // 8, u % 8
                    for hh in range(2):
                        last = mm(psS[:, u % 2, hh * S:(hh + 1) * S],
                                  qstack[0:KROWS, b1.s4, 2 * hp + hh, c * P:(c + 1) * P], kstack[0:KROWS, b1.s4, :],
                                  start=True, stop=True)
                    last.then_inc(sm["max_scored"], 1)
                if active(b3):
                    if u == 0:
                        wait(pe, f"m_stacked{b3.s2}", 16 * b3.half + 16)
                    g, kc, i = u // 8, u // 4 % 2, u % 4
                    wait(pe, "exp_done", UNITS * b3.n + u - 1)
                    heads = qstack[0:KROWS + MROWS, b3.s4, 8 * g + i:8 * g + i + 5:4, :]
                    mm(psT[:, u % 2, :], kstack[0:KROWS + MROWS, b3.s4, kc * P:(kc + 1) * P], heads,
                       start=True, stop=True).then_inc(sm["scored"], 1)
                    if u % 4 == 1 and u > 4:
                        pv(u // 4 - 1)
            if active(b3):
                pv(3)

        pipeline(pe, step)

    @block.scalar
    def _(act):
        copy = nc.scalar.copy
        act.wait_ge(sm["consts_made"], 1)
        act.wait_ge(sm["wc_product"], 1)
        for oc in range(DC):
            last = copy(wc[:, oc, :], psS[:, oc, 0:D])
        last.then_inc(sm["wc_copied"], 1)
        act.wait_ge(sm["gram_product"], 1)
        for ic in range(DC):
            last = copy(gram[:, ic, :], psS[:, ic, 0:D])
        last.then_inc(sm["gram_copied"], 1)
        act.wait_ge(sm["gram_copied"], 2)
        for g in range(NGROUP):
            act.wait_ge(sm["keymap_product"], g + 1)
            for ic in range(DC):
                nc.scalar.activation(keymap[:, ic, g * GROUP:(g + 1) * GROUP], psS[:, ic, 0:GROUP], ACT.Identity,
                                     bias=uvec[:, ic:ic + 1]).then_inc(sm["keymap_copied"], 1)

        def step(t):
            b = t
            if active(b):
                wait(act, "q_projected", done(b))
                wait(act, "q_stored", done(b.back(2), 16))
                copy(qpart[:, b.s2, 0].rearrange("p c s -> p (c s)"), psB[:, :]).then_inc(sm["q1_cast"], 1)
            b3 = t.back(3)

            def copy_att(g):
                wait(act, "pv_done", 4 * b3.n + 2 * g + 2)
                wait(act, "att_transposed", 2 * b3.n + g - 1)
                copy(att_t[:, g, :], psO[:, g, :]).then_inc(sm["att_copied"], 1)

            for u in range(UNITS):
                if u == 1 and active(t):
                    b = t
                    wait(act, "kv_projected", done(b))
                    wait(act, "pv_done", 4 * (b.n - 3))
                    wait(act, "scored", UNITS * (b.n - 3))
                    copy(vaug[:, b.s4, :, 0:DK], psB[:, S:S + QC * DK].rearrange("p (c d) -> p c d", c=QC))
                    copy(kstack[0:KROWS, b.s4], psB[0:KROWS, 0:S]).then_inc(sm["kv_cast"], 1)
                if u == 3 and active(t):
                    b = t
                    wait(act, "k_rest", done(b))
                    copy(kstack[32:64, b.s4], krest[32:64, b.s2])
                    copy(ksmall[64:80, b.s2], krest[64:80, b.s2]).then_inc(sm["k_mid"], 1)
                if u == 4 and active(t.back(2)):
                    b = t.back(2)
                    wait(act, "m_transposed", done(b))
                    wait(act, f"m_stacked{b.s2}", 16 * b.half)
                    copy(mrows[:, b.s2], psA[0:MROWS * NH * QC, 0:P // 2].bitcast(BF16)).then_inc(sm["m_copied"], 1)
                if u == 5 and active(t.back(5)):
                    b = t.back(5)
                    wait(act, "x2_transposed", done(b))
                    wait(act, "gate_scored", done(b.back(2)))
                    copy(x2t[:, b.s2].rearrange("p c s -> p (c s)"), psB[:, :]).then_inc(sm["x2t_copied"], 1)
                if u == 7 and active(t.back(4)):
                    b = t.back(4)
                    wait(act, "x1_transposed", done(b))
                    wait(act, "cross_scored", done(b.back(2)))
                    copy(x1t[:, b.s2].rearrange("p c s -> p (c s)"), psA[:, :]).then_inc(sm["x1t_copied"], 1)
                if u == 10 and active(t.back(4)):
                    b = t.back(4)
                    wait(act, "cross_masked", done(b))
                    wait(act, "cprob_transposed", done(b.back(2)))
                    wait(act, "y2_ready", done(b.back(2)))
                    for c in range(QC):
                        last = nc.scalar.activation(cprob[:, b.s2, c, :], cscore[:, b.s2, c, :], ACT.Exp,
                                                    bias=cnegmax[:, b.s2, c:c + 1],
                                                    accum_out=csum[:, b.s2, c:c + 1])
                    last.then_inc(sm["cross_exp"], 1)
                if u == 11 and active(t.back(5)):
                    b = t.back(5)
                    wait(act, "gate_max", done(b))
                    wait(act, "comb_ready", done(b.back(2)))
                    for c in range(QC):
                        nc.scalar.activation(gexp[:, b.s2, c, :], logits[:, b.s2, c, :], ACT.Exp,
                                             bias=gneg[:, b.s2, c:c + 1], accum_out=gsum[:, b.s2, c:c + 1])
                        last = nc.scalar.activation(gtop[:, b.s2, c, :], top[:, b.s2, c, 0:2], ACT.Exp,
                                                    bias=gneg[:, b.s2, c:c + 1])
                    last.then_inc(sm["gate_exp"], 1)
                if u == 13 and active(t.back(4)):
                    b = t.back(4)
                    wait(act, "cprob_transposed", done(b))
                    wait(act, "cross_out", done(b.back(2)))
                    copy(cprob_t[:, b.s2], psB[0:SC, 0:S]).then_inc(sm["cprobt_copied"], 1)
                if active(b3):
                    wait(act, "scored", UNITS * b3.n + u + 1)
                    if u % 4 == 0:
                        wait(act, "pv_done", 4 * b3.n + u // 4 - 1)
                    nc.scalar.activation(probs[:, u % PT, :], psT[:, u % 2, :], ACT.Exp, scale=SELF_SCALE
                                         ).then_inc(sm["exp_done"], 1)
                    if u == 11:
                        copy_att(0)
            if active(b3):
                copy_att(1)

        pipeline(act, step)

    @block.vector
    def _(dve):
        v = nc.vector
        v.memset(kstack[KROWS:KROWS + MROWS], 1.0)
        dve.wait_ge(sm["consts_made"], 1)
        dve.wait_ge(sm["setup_loaded"], 16 * (8 + KROWS // DK))
        dve.wait_ge(sm["c_product"], 1)
        v.tensor_tensor(cvec[:, :], psT[:, 0, 0:DC], b2c[:, :], ALU.add).then_inc(sm["wc_copied"], 1)
        dve.wait_ge(sm["gram_product"], 1)
        v.tensor_copy(uvec[:, :], psT[:, 1, 0:DC])
        v.tensor_copy(cc[:, :], psO[0:1, 0, 0:1]).then_inc(sm["gram_copied"], 1)
        dve.wait_ge(sm["gram_copied"], 2)
        for g in range(NGROUP):
            dve.wait_ge(sm["keymap_product"], g + 1)
            v.tensor_scalar(keybias[:, g * GROUP:(g + 1) * GROUP], psT[0:1, 0, 0:GROUP], cc[:, :], None, ALU.add
                            ).then_inc(sm["keymap_copied"], 1)

        def norm(x, mv, rs, y, b, name):
            for c in range(QC):
                last = v.tensor_scalar(x[:, b.s2, c, 0:D], y[:, b.s2, c, :], mv[:, b.s2, c, 0:1], rs[:, b.s2, c:c + 1],
                                       ALU.subtract, ALU.mult)
            last.then_inc(sm[name], 1)

        def stats(y, out, b, name):
            for c in range(QC):
                last = v.bn_stats(out[:, b.s2, c, :], y[:, b.s2, c, :])
            last.then_inc(sm[name], 1)

        def moments(out, mv, b, name):
            for c in range(QC):
                last = v.bn_aggr(mv[:, b.s2, c, :], out[:, b.s2, c, :])
            last.then_inc(sm[name], 1)

        def att_norm(b, g):
            wait(dve, "att_transposed", 2 * b.n + g + 1)
            view = psA[:, :].rearrange("p (c j k) -> p c j k", c=QC, k=32)
            rec = rden[:, g].rearrange("p (c j) -> p c j", c=QC)
            wait(dve, "y1_ready", done(b.back(2)))
            v.reciprocal(rec, view[:, :, :, DK]).then_inc(sm["den_ready"], 1)
            wait(dve, "den_ready", 2 * b.n + g + 1)
            v.tensor_tensor(att[:, b.s2, :, g * P:(g + 1) * P].rearrange("p c (j k) -> p c j k", k=DK),
                            view[:, :, :, 0:DK], rec.unsqueeze(3).to_broadcast([P, QC, 8, DK]), ALU.mult
                            ).then_inc(sm["att_normed"], 1)

        def step(t):
            b = t.back(4)
            if active(b):
                att_norm(b, 0)
            b1 = t.back(1)
            for u in range(UNITS):
                if u == 0 and active(t.back(5)):
                    wait(dve, "stats2_ready", done(t.back(5)))
                if u == 4 and active(t.back(4)):
                    wait(dve, "stats1_ready", done(t.back(4)))
                if u == 9 and active(t.back(5)):
                    wait(dve, "gate_max", done(t.back(5)))
                if active(b1):
                    wait(dve, "max_scored", UNITS * b1.n + u + 1)
                    c, hp = u // 8, u % 8
                    v.tensor_reduce(negmax[:, b1.s2, 2 * hp:2 * hp + 2, c],
                                    psS[:, u % 2, :].rearrange("p (h k) -> p h k", h=2), AX.X, ALU.max, negate=True
                                    ).then_inc(sm["max_reduced"], 1)
                if u == 0 and active(t.back(5)):
                    moments(stats2, mv2, t.back(5), "var2_ready")
                if u == 2 and active(t.back(5)):
                    b = t.back(5)
                    wait(dve, "rstd2_ready", done(b, 2))
                    wait(dve, f"x2_stored{b.s2}", 16 * b.half)
                    wait(dve, "x2_transposed", done(b.back(2)))
                    wait(dve, f"dispatched{b.s2}", 2 * QC * 16 * b.half)
                    if not b.fixed or b.n >= 2:
                        v.tensor_scalar(x2[:, b.s2, :, D + E], x2[:, b.s2, :, D + E], float(2 * S), None, ALU.add)
                    norm(x2, mv2, rstd2, y2, b, "x2_ready")
                if u == 0 and active(t):
                    b = t
                    wait(dve, "q1_cast", done(b))
                    wait(dve, "q_split", done(b.back(2), 2))
                    v.tensor_tensor(qrest[:, b.s2].rearrange("p c s -> p (c s)"), psB[:, :],
                                    qpart[:, b.s2, 0].rearrange("p c s -> p (c s)"), ALU.subtract
                                    ).then_inc(sm["q_rest"], 1)
                if u == 0 and active(t.back(4)):
                    att_norm(t.back(4), 1)
                if u == 1 and active(t.back(2)):
                    b = t.back(2)
                    wait(dve, "max_reduced", UNITS * (b.n + 1))
                    wait(dve, "m_transposed", done(b.back(2)))
                    m, r, part = negmax[:, b.s2], mrest[:, b.s2], mpart[:, b.s2]
                    v.tensor_copy(part[:, 0], m).then_inc(sm["m_link"], 1)
                    wait(dve, "m_link", 3 * b.n + 1)
                    v.tensor_tensor(r, m, part[:, 0], ALU.subtract).then_inc(sm["m_link"], 1)
                    wait(dve, "m_link", 3 * b.n + 2)
                    v.tensor_copy(part[:, 1], r).then_inc(sm["m_link"], 1)
                    wait(dve, "m_link", 3 * b.n + 3)
                    v.tensor_tensor(part[:, 2], r, part[:, 1], ALU.subtract).then_inc(sm["m_split"], 1)
                if u == 2 and active(t):
                    b = t
                    wait(dve, "kv_cast", done(b))
                    wait(dve, "k_split", done(b.back(2)))
                    v.tensor_tensor(krest[0:KROWS, b.s2], psB[0:KROWS, 0:S], kstack[0:KROWS, b.s4], ALU.subtract
                                    ).then_inc(sm["k_rest"], 1)
                if u == 4 and active(t):
                    b = t
                    wait(dve, "k_mid", done(b))
                    v.tensor_tensor(kstack[64:80, b.s4], krest[64:80, b.s2], ksmall[64:80, b.s2], ALU.subtract
                                    ).then_inc(sm["k_split"], 1)
                if u == 3 and active(t.back(4)):
                    b = t.back(4)
                    wait(dve, "y1_ready", done(b))
                    stats(y1, stats1, b, "stats1_ready")
                if u == 4 and active(t.back(4)):
                    moments(stats1, mv1, t.back(4), "var1_ready")
                if u == 5 and active(t.back(4)):
                    b = t.back(4)
                    wait(dve, "rstd1_ready", done(b, 2))
                    norm(x1, mv1, rstd1, y1, b, "x1_ready")
                if u == 8 and active(t.back(5)):
                    b = t.back(5)
                    wait(dve, "gate_scored", done(b))
                    wait(dve, "gate_exp", done(b.back(2)))
                    v.tensor_copy(logits[:, b.s2], psB[:, 0:QC * E].rearrange("p (c e) -> p c e", c=QC)
                                  ).then_inc(sm["gate_link"], 1)
                    dve.wait_ge(sm["gate_link"], done(b, 7, 1))
                    v.tensor_reduce(gneg[:, b.s2], logits[:, b.s2], AX.X, ALU.max, negate=True)
                    for c in range(QC):
                        last = v.max(top[:, b.s2, c, :], logits[:, b.s2, c, :])
                    last.then_inc(sm["gate_max"], 1)
                if u == 9 and active(t.back(5)):
                    b = t.back(5)
                    for c in range(QC):
                        last = v.max_index(topi[:, b.s2, c, :], top[:, b.s2, c, :], logits[:, b.s2, c, :])
                    last.then_inc(sm["gate_link"], 1)
                if u == 9 and active(t.back(4)):
                    b = t.back(4)
                    wait(dve, "cross_scored", done(b))
                    wait(dve, "cross_exp", done(b.back(2)))
                    v.scalar_tensor_tensor(cscore[:, b.s2], psA[:, 0:QC * SC].rearrange("p (c k) -> p c k", c=QC),
                                           CROSS_SCALE, mask[:, :, :], ALU.mult, ALU.add).then_inc(sm["score_link"], 1)
                    wait(dve, "score_link", done(b))
                    v.tensor_reduce(cnegmax[:, b.s2], cscore[:, b.s2], AX.X, ALU.max, negate=True
                                    ).then_inc(sm["cross_masked"], 1)
                if u == 12 and active(t.back(5)):
                    b = t.back(5)
                    wait(dve, "gate_exp", done(b))
                    link = lambda k: dve.wait_ge(sm["gate_link"], done(b, 7, k))
                    link(2)
                    v.tensor_copy(topf[:, b.s2], topi[:, b.s2, :, 0:2]).then_inc(sm["gate_link"], 1)
                    v.scalar_tensor_tensor(gden[:, b.s2], gsum[:, b.s2], GATE_EPS, gtop[:, b.s2, :, 0], ALU.mult,
                                           ALU.add).then_inc(sm["gate_link"], 1)
                    link(4)
                    v.tensor_tensor(gden[:, b.s2], gden[:, b.s2], gtop[:, b.s2, :, 1], ALU.add
                                    ).then_inc(sm["gate_link"], 1)
                    for c in range(QC):
                        for k in range(2):
                            last = v.tensor_scalar(hot[:, b.s2, c, k, :], iota_e[:, c, :], topf[:, b.s2, c, k:k + 1],
                                                   None, ALU.is_equal)
                    last.then_inc(sm["gate_link"], 1)
                    link(5)
                    v.reciprocal(gden[:, b.s2], gden[:, b.s2]).then_inc(sm["gate_link"], 1)
                    link(6)
                    wait(dve, "counted", done(b.back(2)))
                    v.tensor_tensor(hotsum[:, b.s2], hot[:, b.s2, :, 0, :], hot[:, b.s2, :, 1, :], ALU.add
                                    ).then_inc(sm["hot_ready"], 1)
                    link(7)
                    wait(dve, "hot_ready", done(b))
                    for c in range(QC):
                        last = v.scalar_tensor_tensor(x2[:, b.s2, c, D:D + E], gexp[:, b.s2, c, :],
                                                      gden[:, b.s2, c:c + 1], hotsum[:, b.s2, c, :],
                                                      ALU.mult, ALU.mult)
                    last.then_inc(sm["comb_ready"], 1)
            b = t.back(5)
            if active(b):
                wait(dve, "counted", done(b))
                wait(dve, "slots_ready", done(b.back(1)))
                count = psB[:, 0:3 * E].rearrange("p (c e) -> p c e", e=E)
                now, then = base[:, b.s2, :], base[:, 1 - b.s2, :]
                v.tensor_tensor(place[:, b.s2], count[:, 0:QC, :], now.unsqueeze(1).to_broadcast([P, QC, E]), ALU.add)
                v.tensor_tensor(then, count[:, QC, :], now, ALU.add).then_inc(sm["slot_link"], 1)
                wait(dve, "slot_link", 3 * b.n + 1)
                v.tensor_tensor(chosen[:, b.s2], hot[:, b.s2], place[:, b.s2].unsqueeze(2).to_broadcast([P, QC, 2, E]),
                                ALU.mult).then_inc(sm["slot_link"], 1)
                wait(dve, "slot_link", 3 * b.n + 2)
                v.tensor_reduce(slotf[:, b.s2], chosen[:, b.s2], AX.X, ALU.add).then_inc(sm["slot_link"], 1)
                wait(dve, "slot_link", 3 * b.n + 3)
                v.tensor_copy(slots[:, b.s2], slotf[:, b.s2].rearrange("p c k -> p (c k)")).then_inc(sm["slots_ready"], 1)
            b = t.back(4)
            if active(b):
                wait(dve, "cross_exp", done(b))
                v.reciprocal(crec[:, b.s2], csum[:, b.s2]).then_inc(sm["crec_ready"], 1)
                wait(dve, "cross_out", done(b))
                wait(dve, "crec_ready", done(b))
                for c in range(QC):
                    last = v.scalar_tensor_tensor(y2[:, b.s2, c, :], psA[:, c * D:(c + 1) * D], crec[:, b.s2, c:c + 1],
                                                  x1[:, b.s2, c, :], ALU.mult, ALU.add)
                last.then_inc(sm["y2_ready"], 1)
                wait(dve, "y2_ready", done(b))
                stats(y2, stats2, b, "stats2_ready")

        pipeline(dve, step)


def experts(nc, ctx, io, dram):
    base = dram["base"]
    T, D = dram["sum"].shape
    T -= P
    E, _, H2 = io["f1_t"].shape
    H = H2 // 2
    DC, HC = D // P, H // P
    ROW = D + E + 1
    STRIDE = dram["stride"]
    TILES = 2 * T // P + E

    def sb(name, shape, dt=F32):
        return ctx.enter_context(nc.sbuf_tensor(name, shape, dt))

    def ps(name, shape, dt=F32):
        return ctx.enter_context(nc.psum_tensor(name, shape, dt))

    I32 = mybir.dt.int32
    ident = sb("ident2", [P, P])
    w1 = sb("f_w1", [P, DC, E * H2])
    b1 = sb("f_b1", [P, E * H2])
    wo = sb("f_wo", [P, HC, D])
    bo = sb("f_bo", [P, D])
    cnt = sb("cnt", [P, E])
    cnti = sb("cnti", [P, E], I32)
    ntile = sb("ntile", [P, E])
    upto = sb("upto", [P, E])
    skip = sb("skip", [P, E])
    listbase = sb("listbase", [P, E])
    number = sb("number", [P, TILES])
    past = sb("past", [P, TILES])
    rowf = sb("rowf", [P, TILES])
    expf = sb("expf", [P, TILES])
    row_tab = sb("row_tab", [P, TILES], I32)
    exp_tab = sb("exp_tab", [P, TILES], I32)
    pad_place = sb("pad_place", [P, E])
    pad_rows = sb("pad_rows", [P, E], U32)
    pad = sb("pad", [P, ROW])
    partition = sb("partition", [P, 1])
    xe = sb("xe", [P, 4, ROW])
    xet = sb("xet", [P, 2, DC, P])
    hb = sb("hb", [P, 2, H])
    ha = sb("ha", [P, 2, H])
    sig = sb("sig", [P, 2, H])
    g = sb("g", [P, 2, H])
    gt = sb("gt", [P, 2, HC, P])
    yb = sb("yb", [P, 2, D])
    y = sb("y", [P, 2, D])
    weight = sb("weight", [P, 4, 1])
    token = sb("token", [P, 4], U32)

    psX = ps("psX", [P, 512])
    psG = ps("psG", [P, 512])
    psHa = ps("psHa", [P, 2, 512])
    psHb = ps("psHb", [P, 2, 512])
    psY = ps("psY", [P, 2, 512])

    names = ["weights_loaded", "consts_made2", "pads_made", "pads_written", "table_link", "tables_ready", "pad_rows_ready",
             "xe_loaded0", "xe_loaded1", "xe_loaded2", "xe_loaded3",
             "x_transposed", "b_product", "a_product", "g_transposed", "y_product",
             "xet_copied", "sig_ready", "gt_copied",
             "hb_ready", "ha_ready", "g_ready", "yb_ready", "y_ready", "token_ready", "summed"]
    sm = {n: ctx.enter_context(nc.semaphore(n)) for n in names}

    def wait(eng, name, value):
        if isinstance(value, int) and value <= 0:
            return
        eng.wait_ge(sm[name], value)

    def done(i, per=1):
        return per * (i.n + 1)

    def active(i):
        return not i.fixed or 0 <= i.n < TILES

    def pipeline(eng, step):
        for r in range(8):
            step(Step(0, r))
        with eng.Fori(2, TILES // 4) as j:
            for r in range(4):
                step(Step(j, r))
        for r in range(4):
            step(Step(TILES // 4, r))

    block = ctx.enter_context(nc.Block())

    @block.sync
    def _(sp):
        sp.dma_start(bo[:, :], io["bo"].unsqueeze(0).to_broadcast([P, D])).then_inc(sm["weights_loaded"], 16)
        sp.dma_start(wo[:, :, :], io["wo_t"].rearrange("(c p) d -> p c d", p=P)).then_inc(sm["weights_loaded"], 16)
        for e in range(E):
            sp.dma_start(w1[:, :, e * H2:(e + 1) * H2], io["f1_t"][e].rearrange("(c p) h -> p c h", p=P)
                         ).then_inc(sm["weights_loaded"], 16)
            sp.dma_start(b1[:, e * H2:(e + 1) * H2], io["f1_b"][e].unsqueeze(0).to_broadcast([P, H2])
                         ).then_inc(sm["weights_loaded"], 16)
        sp.wait_ge(sm["tables_ready"], 2)
        sp.wait_ge(sm["pads_written"], 16 * (E + 2))

        def step(t):
            if active(t):
                wait(sp, "y_ready", done(t.back(4)))
                row = sp.value_load(row_tab[0:1, bass.ds(t.n, 1)], min_val=0, max_val=E * STRIDE)
                sp.dma_start(xe[:, t.s4], dram["lists"][bass.ds(row, P), :]).then_inc(sm[f"xe_loaded{t.s4}"], 16)

        pipeline(sp, step)

    @block.gpsimd
    def _(pool):
        pool.memset(ident[:, :], 0.0)
        pool.memset(pad[:, :], 0.0).then_inc(sm["consts_made2"], 1)
        pool.iota(partition[:, :], pattern=[[0, 1]], base=0, channel_multiplier=1, allow_small_or_imprecise_dtypes=True)
        pool.iota(listbase[:, :], pattern=[[STRIDE, E]], base=0, channel_multiplier=0,
                  allow_small_or_imprecise_dtypes=True)
        pool.iota(number[:, :], pattern=[[1, TILES]], base=0, channel_multiplier=0, allow_small_or_imprecise_dtypes=True)
        pool.wait_ge(sm["consts_made2"], 1)
        pool.affine_select(out=ident[:, :], in_=ident[:, :], compare_op=ALU.not_equal, fill=1.0, base=0,
                           pattern=[[-1, P]], channel_multiplier=1)
        pool.iota(pad[:, ROW - 1:ROW], pattern=[[0, 1]], base=T, channel_multiplier=1,
                  allow_small_or_imprecise_dtypes=True).then_inc(sm["consts_made2"], 1)
        pool.wait_ge(sm["consts_made2"], 2)
        pool.dma_start(dram["lists"][E * STRIDE:E * STRIDE + P, :], pad[:, :]).then_inc(sm["pads_written"], 16)
        pool.dma_start(dram["sum"][T:T + P, :], pad[:, 0:D]).then_inc(sm["pads_written"], 16)
        pool.wait_ge(sm["pad_rows_ready"], 1)
        for e in range(E):
            pool.indirect_dma_start(out=dram["lists"], out_offset=bass.IndirectOffsetOnAxis(
                ap=pad_rows[:, e:e + 1], axis=0), in_=pad[:, :], in_offset=None).then_inc(sm["pads_written"], 16)

        def step(t):
            i, o = t.back(2), t.back(3)
            if active(i):
                wait(pool, "y_ready", done(o))
                wait(pool, "summed", 16 * o.n)
                wait(pool, "yb_ready", done(i))
                pool.tensor_tensor(y[:, i.s2], yb[:, i.s2], weight[:, i.s4].to_broadcast([P, D]), ALU.mult
                                   ).then_inc(sm["y_ready"], 1)
            if active(o):
                if o.fixed and not active(i):
                    wait(pool, "y_ready", done(o))
                    wait(pool, "summed", 16 * o.n)
                pool.indirect_dma_start(out=dram["sum"], out_offset=bass.IndirectOffsetOnAxis(
                    ap=token[:, o.s4:o.s4 + 1], axis=0), in_=y[:, o.s2], in_offset=None, compute_op=ALU.add
                    ).then_inc(sm["summed"], 16)

        pipeline(pool, step)
        pool.wait_ge(sm["summed"], 16 * TILES)

    @block.tensor
    def _(pe):
        mm = nc.tensor.matmul
        pe.wait_ge(sm["consts_made2"], 2)
        pe.wait_ge(sm["tables_ready"], 2)
        pe.wait_ge(sm["weights_loaded"], 16 * (2 + 2 * E))

        def step(t):
            i = t
            if active(i):
                wait(pe, f"xe_loaded{i.s4}", 16 * (i.j + i.r // 4) + 16)
                wait(pe, "xet_copied", done(i.back(1)))
                for k in range(DC):
                    last = nc.tensor.transpose(psX[:, k * P:(k + 1) * P], xe[:, i.s4, k * P:(k + 1) * P], ident[:, :])
                last.then_inc(sm["x_transposed"], 1)
            i = t.back(1)
            if active(i):
                e = pe.value_load(exp_tab[0:1, bass.ds(i.n, 1)], min_val=0, max_val=E - 1)
                wait(pe, "xet_copied", done(i))
                wait(pe, "hb_ready", done(i.back(2)))
                for k in range(DC):
                    last = mm(psHb[:, i.s2, :], xet[:, i.s2, k, :], w1[:, k, bass.ds(e * H2 + H, H)],
                              start=k == 0, stop=k == DC - 1)
                last.then_inc(sm["b_product"], 1)
            o = t.back(2)
            if active(o):
                wait(pe, "g_ready", done(o))
                wait(pe, "gt_copied", done(o.back(1)))
                for k in range(HC):
                    last = nc.tensor.transpose(psG[:, k * P:(k + 1) * P], g[:, o.s2, k * P:(k + 1) * P], ident[:, :])
                last.then_inc(sm["g_transposed"], 1)
            if active(i):
                wait(pe, "ha_ready", done(i.back(2)))
                for k in range(DC):
                    last = mm(psHa[:, i.s2, :], xet[:, i.s2, k, :], w1[:, k, bass.ds(e * H2, H)],
                              start=k == 0, stop=k == DC - 1)
                last.then_inc(sm["a_product"], 1)
            if active(o):
                wait(pe, "gt_copied", done(o))
                wait(pe, "yb_ready", done(o.back(2)))
                for k in range(HC):
                    last = mm(psY[:, o.s2, 0:D], gt[:, o.s2, k, :], wo[:, k, :], start=k == 0, stop=k == HC - 1)
                last.then_inc(sm["y_product"], 1)

        pipeline(pe, step)

    @block.scalar
    def _(act):
        copy = nc.scalar.copy

        def step(t):
            i = t
            if active(i):
                wait(act, "x_transposed", done(i))
                wait(act, "a_product", done(i.back(2)))
                copy(xet[:, i.s2].rearrange("p c s -> p (c s)"), psX[:, 0:D]).then_inc(sm["xet_copied"], 1)
            o = t.back(2)
            if active(o):
                wait(act, "g_transposed", done(o))
                wait(act, "y_product", done(o.back(2)))
                copy(gt[:, o.s2].rearrange("p c s -> p (c s)"), psG[:, :]).then_inc(sm["gt_copied"], 1)
            i = t.back(1)
            if active(i):
                wait(act, "hb_ready", done(i))
                wait(act, "g_ready", done(i.back(2)))
                nc.scalar.activation(sig[:, i.s2], hb[:, i.s2], ACT.Sigmoid).then_inc(sm["sig_ready"], 1)

        pipeline(act, step)

    @block.vector
    def _(dve):
        v = nc.vector
        links = 0

        def link(ins):
            nonlocal links
            links += 1
            ins.then_inc(sm["table_link"], 1)
            dve.wait_ge(sm["table_link"], links)

        dve.wait_ge(sm["consts_made2"], 2)
        last = base[:, 0, :]
        link(v.tensor_scalar(pad_place[:, :], last, partition[:, :], None, ALU.add))
        v.tensor_copy(pad_rows[:, :], pad_place[:, :]).then_inc(sm["pad_rows_ready"], 1)
        link(v.tensor_tensor(cnt[:, :], last, listbase[:, :], ALU.subtract))
        link(v.tensor_scalar(cnti[:, :], cnt[:, :], float(P - 1), None, ALU.add))
        link(v.tensor_single_scalar(cnti[:, :], cnti[:, :], 7, ALU.logical_shift_right))
        link(v.tensor_copy(ntile[:, :], cnti[:, :]))
        link(v.tensor_copy(upto[:, 0:1], ntile[:, 0:1]))
        for e in range(1, E):
            link(v.tensor_tensor(upto[:, e:e + 1], upto[:, e - 1:e], ntile[:, e:e + 1], ALU.add))
        link(v.tensor_scalar(skip[:, :], ntile[:, :], -float(P), float(STRIDE), ALU.mult, ALU.add))
        link(v.tensor_scalar(rowf[:, :], number[:, :], float(P), None, ALU.mult))
        link(v.memset(expf[:, :], 0.0))
        for e in range(E):
            link(v.tensor_scalar(past[:, :], number[:, :], upto[:, e:e + 1], None, ALU.is_ge))
            link(v.scalar_tensor_tensor(rowf[:, :], past[:, :], skip[:, e:e + 1], rowf[:, :], ALU.mult, ALU.add))
            link(v.tensor_tensor(expf[:, :], expf[:, :], past[:, :], ALU.add))
        v.tensor_scalar(row_tab[:, :], rowf[:, :], float(E * STRIDE), None, ALU.min).then_inc(sm["tables_ready"], 1)
        v.tensor_scalar(exp_tab[:, :], expf[:, :], float(E - 1), None, ALU.min).then_inc(sm["tables_ready"], 1)
        dve.wait_ge(sm["tables_ready"], 2)
        dve.wait_ge(sm["weights_loaded"], 16 * (2 + 2 * E))

        def step(t):
            i = t.back(1)
            if active(i):
                e = dve.value_load(exp_tab[0:1, bass.ds(i.n, 1)], min_val=0, max_val=E - 1)
                wait(dve, f"xe_loaded{i.s4}", 16 * (i.j + i.r // 4) + 16)
                wait(dve, "summed", 16 * (i.n - 3))
                wait(dve, "b_product", done(i))
                wait(dve, "sig_ready", done(i.back(2)))
                v.tensor_tensor(hb[:, i.s2], psHb[:, i.s2, :], b1[:, bass.ds(e * H2 + H, H)], ALU.add
                                ).then_inc(sm["hb_ready"], 1)
                v.tensor_copy(token[:, i.s4:i.s4 + 1], xe[:, i.s4, ROW - 1:ROW])
                v.tensor_copy(weight[:, i.s4], xe[:, i.s4, bass.ds(e + D, 1)]).then_inc(sm["token_ready"], 1)
                wait(dve, "a_product", done(i))
                wait(dve, "g_ready", done(i.back(2)))
                v.tensor_tensor(ha[:, i.s2], psHa[:, i.s2, :], b1[:, bass.ds(e * H2, H)], ALU.add
                                ).then_inc(sm["ha_ready"], 1)
            o = t.back(2)
            if active(o):
                wait(dve, "y_product", done(o))
                wait(dve, "y_ready", done(o.back(2)))
                v.tensor_tensor(yb[:, o.s2], psY[:, o.s2, 0:D], bo[:, :], ALU.add).then_inc(sm["yb_ready"], 1)
            if active(i):
                wait(dve, "ha_ready", done(i))
                wait(dve, "sig_ready", done(i))
                wait(dve, "g_transposed", done(i.back(2)))
                v.tensor_tensor(g[:, i.s2], ha[:, i.s2], sig[:, i.s2], ALU.mult).then_inc(sm["g_ready"], 1)

        pipeline(dve, step)


def final_norm(nc, ctx, io, dram):
    B, S, D = io["x"].shape
    QC = S // P

    def sb(name, shape, dt=F32):
        return ctx.enter_context(nc.sbuf_tensor(name, shape, dt))

    total = sb("total", [P, 4, QC, D])
    stats = sb("stats3", [P, 4, QC, 6])
    mv = sb("mv3", [P, 4, QC, 2])
    vare = sb("vare3", [P, 4, QC])
    rstd = sb("rstd3", [P, 4, QC])
    eps_c = sb("eps3", [P, QC])
    neg_half = sb("neg_half3", [P, QC])
    result = sb("result", [P, 4, QC, D])
    names = ["consts_made3", "stats3_ready", "var3_ready", "rstd3_ready", "normed"]
    names += [f"total_loaded{s}" for s in range(4)] + [f"result_stored{s}" for s in range(4)]
    sm = {n: ctx.enter_context(nc.semaphore(n)) for n in names}

    def wait(eng, name, value):
        if isinstance(value, int) and value <= 0:
            return
        eng.wait_ge(sm[name], value)

    def active(b):
        return not b.fixed or 0 <= b.n < B

    def pipeline(eng, step):
        for r in range(8):
            step(Step(0, r))
        with eng.Fori(2, B // 4) as j:
            for r in range(4):
                step(Step(j, r))
        for r in range(3):
            step(Step(B // 4, r))

    block = ctx.enter_context(nc.Block())
    rows = dram["sum"][0:B * S, :].rearrange("(b s) d -> b s d", s=S)

    @block.sync
    def _(sp):
        def step(t):
            if active(t):
                wait(sp, "normed", t.n - 3)
                sp.dma_start(total[:, t.s4], rows[bass.ds(t.n, 1)].rearrange("o (c p) d -> p (o c) d", p=P)
                             ).then_inc(sm[f"total_loaded{t.s4}"], 16)

        pipeline(sp, step)

    @block.scalar
    def _(act):
        def step(t):
            b = t.back(2)
            if active(b):
                wait(act, "normed", b.n + 1)
                act.dma_start(dram["out"][bass.ds(b.n, 1)].rearrange("o (c p) d -> p (o c) d", p=P), result[:, b.s4]
                              ).then_inc(sm[f"result_stored{b.s4}"], 16)

        pipeline(act, step)
        for s in range(4):
            act.wait_ge(sm[f"result_stored{s}"], 16 * (B // 4))

    @block.gpsimd
    def _(pool):
        pool.memset(eps_c[:, :], EPS)
        pool.memset(neg_half[:, :], -0.5).then_inc(sm["consts_made3"], 1)
        pool.wait_ge(sm["consts_made3"], 1)

        def step(t):
            b = t.back(1)
            if active(b):
                wait(pool, "var3_ready", b.n + 1)
                pool.tensor_tensor(vare[:, b.s4], mv[:, b.s4, :, 1], eps_c[:, :], ALU.add).then_inc(sm["rstd3_ready"], 1)
                wait(pool, "rstd3_ready", 2 * b.n + 1)
                pool.tensor_tensor(rstd[:, b.s4], vare[:, b.s4], neg_half[:, :], ALU.pow).then_inc(sm["rstd3_ready"], 1)

        pipeline(pool, step)

    @block.vector
    def _(dve):
        v = nc.vector

        def step(t):
            if active(t):
                wait(dve, f"total_loaded{t.s4}", 16 * (t.j + t.r // 4) + 16)
                for c in range(QC):
                    last = v.bn_stats(stats[:, t.s4, c, :], total[:, t.s4, c, :])
                last.then_inc(sm["stats3_ready"], 1)
                wait(dve, "stats3_ready", t.n + 1)
            b = t.back(2)
            if active(b):
                wait(dve, "rstd3_ready", 2 * b.n + 2)
                wait(dve, f"result_stored{b.s4}", 16 * (b.j + b.r // 4))
                for c in range(QC):
                    last = v.tensor_scalar(result[:, b.s4, c, :], total[:, b.s4, c, :], mv[:, b.s4, c, 0:1],
                                           rstd[:, b.s4, c:c + 1], ALU.subtract, ALU.mult)
                last.then_inc(sm["normed"], 1)
            if active(t):
                for c in range(QC):
                    last = v.bn_aggr(mv[:, t.s4, c, :], stats[:, t.s4, c, :])
                last.then_inc(sm["var3_ready"], 1)

        pipeline(dve, step)


def decoder_layer(nc, io, out):
    B, S, D = io["x"].shape
    E = io["wg_t"].shape[1]
    T = B * S
    stride = T + P
    with ExitStack() as ctx:
        dram = {
            "q": nc.dram_tensor("q_parts", (2, 3, D, S), BF16, kind="Internal").ap(),
            "sum": nc.dram_tensor("sums", (T + P, D), F32, kind="Internal").ap(),
            "lists": nc.dram_tensor("lists", (E * stride + P, D + E + 1), F32, kind="Internal").ap(),
            "base": ctx.enter_context(nc.sbuf_tensor("base", [P, 2, E], F32)),
            "stride": stride,
            "out": out,
        }
        for phase in (attention, experts, final_norm):
            with ExitStack() as own:
                phase(nc, own, io, dram)


def kernel(**inputs):
    from concourse import bacc
    from concourse.bass_utils import run_bass_kernel_spmd

    a = {k: np.asarray(v) for k, v in inputs.items()}
    D = a["x"].shape[2]
    laid = {
        "x": a["x"],
        "x_t": a["x"].transpose(0, 2, 1),
        "context": a["ctx_1024"],
        "context_t": a["ctx_1024"].reshape(-1, D).T,
        "mask": a["fside_1xSxS2_0"][0],
        "wq_t": a["L0_attn_Wq"].T,
        "wk_t": a["L0_attn_Wk"].T,
        "wv_t": a["L0_attn_Wv"].T,
        "w1": a["L0_xattn_W1"],
        "w2_t": a["L0_xattn_W2"].T,
        "b1": a["L0_xattn_b1"].reshape(-1, P).T,
        "b2": a["L0_xattn_b2"].reshape(-1, P).T,
        "wg_t": a["L0_ffn_Wg"].T,
        "f1_t": a["L0_ffn_W1"].transpose(0, 2, 1),
        "f1_b": a["L0_ffn_b1"],
        "wo_t": a["L0_ffn_Wo"].T,
        "bo": a["L0_ffn_bo"],
    }
    nc = bacc.Bacc("TRN2", target_bir_lowering=False, num_devices=1)
    arrays, io = {}, {}
    for name, array in laid.items():
        array = np.ascontiguousarray(array)
        arrays[f"in_{name}"] = array
        io[name] = nc.dram_tensor(f"in_{name}", array.shape, mybir.dt.from_np(array.dtype), kind="ExternalInput").ap()
    out = nc.dram_tensor("out", a["x"].shape, F32, kind="ExternalOutput").ap()
    decoder_layer(nc, io, out)
    result = run_bass_kernel_spmd(nc, [arrays], core_ids=[0])
    return result.results[0]["out"]
```

```python
from contextlib import ExitStack

import numpy as np

import concourse.bass as bass
from concourse import mybir

F32 = mybir.dt.float32
BF16 = mybir.dt.bfloat16
F32R = mybir.dt.float32r
U32 = mybir.dt.uint32
ALU = mybir.AluOpType
ACT = mybir.ActivationFunctionType
AX = mybir.AxisListType

P = 128
EPS = 1e-5
GATE_EPS = 1e-9
QPART = (0, 1, 0, 1, 0, 2)
KROWS = 96
MROWS = 3


class Step:

    def __init__(self, j, r):
        self.j, self.r = j, r

    def back(self, k):
        return Step(self.j, self.r - k)

    @property
    def fixed(self):
        return isinstance(self.j, int)

    @property
    def n(self):
        return 4 * self.j + self.r

    @property
    def half(self):
        return 2 * self.j + self.r // 2

    @property
    def s2(self):
        return self.r % 2

    @property
    def s4(self):
        return self.r % 4


def attention(nc, ctx, io, dram):
    B, S, D = io["x"].shape
    SC = io["context"].shape[1]
    NH = 16
    DK = D // NH
    DC = D // P
    QC = S // P
    E = io["wg_t"].shape[1]
    UNITS = 16
    SELF_SCALE = DK ** -0.5
    CROSS_SCALE = D ** -0.5
    GROUP = 4 * SC
    NGROUP = B // 4
    STRIDE = dram["stride"]

    def sb(name, shape, dt=F32):
        return ctx.enter_context(nc.sbuf_tensor(name, shape, dt))

    def ps(name, shape, dt=F32):
        return ctx.enter_context(nc.psum_tensor(name, shape, dt))

    def sem(name):
        return ctx.enter_context(nc.semaphore(name))

    qstack = sb("qstack", [P, 4, NH, S], BF16)
    with (nc.sbuf_tensor("w1", [P, DC, D], F32) as w1, nc.sbuf_tensor("w2t", [P, DC, D], F32) as w2t,
          nc.sbuf_tensor("wc", [P, DC, D], F32) as wc, nc.sbuf_tensor("gram", [P, DC, D], F32) as gram,
          nc.sbuf_tensor("ctx_t", [P, DC, 2, GROUP], F32) as ctx_t):
        pass
    PT = 8
    probs = sb("probs", [P, PT, 2 * S])
    xt = sb("xt", [P, 2, DC, S])
    qpart = sb("qpart", [P, 2, 3, DC, S], BF16)
    qrest = sb("qrest", [P, 2, DC, S])
    krest = sb("krest", [P, 2, S])
    kstack = sb("kstack", [P, 4, S], BF16)
    ident = sb("ident", [P, P])
    ident_b = sb("ident_b", [P, P], BF16)
    neg_half = sb("neg_half", [P, QC])
    neg_one = sb("neg_one", [P, QC])
    eps_c = sb("eps_c", [P, QC])
    one_c = sb("one_c", [P, 1])
    wq = sb("wq", [P, DC, D])
    wk = sb("wk", [P, DC, KROWS])
    wv = sb("wv", [P, DC, DK])
    wg = sb("wg", [P, DC, E])
    mask = sb("mask", [P, QC, SC])
    ones_row = sb("ones_row", [1, P])
    iota_e = sb("iota_e", [P, QC, E])
    b1c = sb("b1c", [P, DC])
    b2c = sb("b2c", [P, DC])
    cvec = sb("cvec", [P, DC])
    uvec = sb("uvec", [P, DC])
    c_dot_c = sb("c_dot_c", [1, 1])
    keymap = sb("keymap", [P, DC, B * SC])
    keybias = sb("keybias", [1, B * SC])

    ksmall = sb("ksmall", [P, 2, S], BF16)
    vaug = sb("vaug", [P, 4, QC, 32])
    negmax = sb("negmax", [P, 2, NH, QC])
    mrest = sb("mrest", [P, 2, NH, QC])
    mpart = sb("mpart", [P, 2, MROWS, NH, QC], BF16)
    mrows = sb("mrows", [MROWS * NH * QC, 2, P], BF16)
    att_t = sb("att_t", [P, 2, 2 * S])
    rden = sb("rden", [P, 2, QC * 8])
    att = sb("att", [P, 2, QC, D])
    xres = sb("xres", [P, 2, QC, D])
    y1 = sb("y1", [P, 2, QC, D])
    stats1 = sb("stats1", [P, 2, QC, 6])
    mv1 = sb("mv1", [P, 2, QC, 2])
    vare1 = sb("vare1", [P, 2, QC])
    nmean1 = sb("nmean1", [P, 2, QC])
    rstd1 = sb("rstd1", [P, 2, QC])
    shift1 = sb("shift1", [P, 2, QC])
    x1 = sb("x1", [P, 2, QC, D])
    x1t = sb("x1t", [P, 2, DC, S])
    cscore = sb("cscore", [P, 2, QC, SC])
    cnegmax = sb("cnegmax", [P, 2, QC])
    cprob = sb("cprob", [P, 2, QC, SC])
    csum = sb("csum", [P, 2, QC])
    crec = sb("crec", [P, 2, QC])
    cprob_t = sb("cprob_t", [SC, 2, S])
    ctxv = sb("ctxv", [SC, 2, D])
    y2 = sb("y2", [P, 2, QC, D])
    stats2 = sb("stats2", [P, 2, QC, 6])
    mv2 = sb("mv2", [P, 2, QC, 2])
    vare2 = sb("vare2", [P, 2, QC])
    nmean2 = sb("nmean2", [P, 2, QC])
    rstd2 = sb("rstd2", [P, 2, QC])
    shift2 = sb("shift2", [P, 2, QC])
    ROW = D + E + 1
    x2 = sb("x2", [P, 2, QC, ROW])
    x2t = sb("x2t", [P, 2, DC, S])
    logits = sb("logits", [P, 2, QC, E])
    top = sb("top", [P, 2, QC, 8])
    topi = sb("topi", [P, 2, QC, 8], U32)
    topf = sb("topf", [P, 2, QC, 2])
    gneg = sb("gneg", [P, 2, QC])
    gexp = sb("gexp", [P, 2, QC, E])
    gsum = sb("gsum", [P, 2, QC])
    gtop = sb("gtop", [P, 2, QC, 2])
    gden = sb("gden", [P, 2, QC])
    hot = sb("hot", [P, 2, QC, 2, E])
    hotsum = sb("hotsum", [P, 2, QC, E], BF16)
    before = sb("before", [P, P], BF16)
    all_ones = sb("all_ones", [P, P], BF16)
    place = sb("place", [P, 2, QC, E])
    chosen = sb("chosen", [P, 2, QC, 2, E])
    slotf = sb("slotf", [P, 2, QC, 2])
    slots = sb("slots", [P, 2, QC * 2], U32)
    base = dram["base"]

    psS = ps("psS", [P, 2, 512])
    psT = ps("psT", [P, 2, 512])
    psO = ps("psO", [P, 2, 512])
    psA = ps("psA", [P, 512])
    psB = ps("psB", [P, 512])

    names = [
        "projections_loaded", "setup_loaded", "ctx_group_even", "ctx_group_odd", "consts_made", "wc_product", "c_product", "wc_copied", "gram_product",
        "gram_copied", "keymap_product", "keymap_copied",
        "xt_loaded0", "xt_loaded1", "xres_loaded0", "xres_loaded1", "ctxv_loaded0", "ctxv_loaded1",
        "q_stored", "q_stacked0", "q_stacked1", "m_stacked0", "m_stacked1", "x2_stored0", "x2_stored1",
        "dispatched0", "dispatched1",
        "q_projected", "kv_projected", "max_scored", "m_transposed", "scored", "pv_done", "att_transposed",
        "x1_transposed", "cross_scored", "cprob_transposed", "cross_out", "x2_transposed", "gate_scored", "counted",
        "q1_cast", "kv_cast", "k_mid", "m_copied", "exp_done", "att_copied", "x1t_copied", "cross_exp",
        "cprobt_copied", "x2t_copied", "gate_exp",
        "q_rest", "k_rest", "k_split", "max_reduced", "m_split", "att_normed", "var1_ready", "x1_ready",
        "cross_masked", "y2_ready", "var2_ready", "x2_ready", "gate_max", "hot_ready", "comb_ready", "slots_ready", "slot_link", "stats1_ready",
        "stats2_ready", "den_ready", "m_link", "gate_link", "score_link", "crec_ready",
        "q_split", "y1_ready", "rstd1_ready", "rstd2_ready", "pool_chain",
    ]
    sm = {n: sem(n) for n in names}

    def wait(eng, name, value):
        if isinstance(value, int) and value <= 0:
            return
        eng.wait_ge(sm[name], value)

    def done(b, per=1, k=None):
        k = per if k is None else k
        return per * b.n + k

    def active(b):
        return not b.fixed or 0 <= b.n < B

    def clamp(b):
        return Step(0, B - 1) if b.fixed and b.n >= B else b

    def pipeline(eng, step):
        for r in range(8):
            step(Step(0, r))
        with eng.Fori(2, B // 4) as j:
            for r in range(4):
                step(Step(j, r))
        for r in range(7):
            step(Step(B // 4, r))

    def load_context_group(eng, g):
        name = "ctx_group_odd" if g % 2 else "ctx_group_even"
        eng.dma_start(ctx_t[:, :, g % 2, :],
                      io["context_t"][:, g * GROUP:(g + 1) * GROUP].rearrange("(c p) k -> p c k", p=P)
                      ).then_inc(sm[name], 16)

    def context_group(t, u):
        places = [(0, UNITS)] * 2 + [(n, k) for n in (1, 2) for k in (3, 8, 13)]
        return [g for g in range(NGROUP) if t.fixed and (t.n, u) == places[g]]

    block = ctx.enter_context(nc.Block())

    @block.sync
    def _(sp):
        for dst, src in ((wq, io["wq_t"].rearrange("(c p) o -> p c o", p=P)),
                         (wv, io["wv_t"].rearrange("(c p) o -> p c o", p=P))):
            sp.dma_start(dst[:, :, :], src).then_inc(sm["projections_loaded"], 16)
        for k in range(KROWS // DK):
            sp.dma_start(wk[:, :, k * DK:(k + 1) * DK],
                         io["wk_t"].rearrange("(c p) o -> p c o", p=P)).then_inc(sm["projections_loaded"], 16)

        def load_setup():
            for dst, src in (
                (w1, io["w1"].rearrange("(c p) o -> p c o", p=P)), (w2t, io["w2_t"].rearrange("(c p) o -> p c o", p=P)),
                (wg, io["wg_t"].rearrange("(c p) o -> p c o", p=P)), (mask, io["mask"].rearrange("(c p) k -> p c k", p=P)),
            ):
                sp.dma_start(dst[:, :, :], src).then_inc(sm["setup_loaded"], 16)
            for dst, src in ((b1c, io["b1"]), (b2c, io["b2"])):
                sp.dma_start(dst[:, :], src).then_inc(sm["setup_loaded"], 16)
            for g in range(2):
                load_context_group(sp, g)

        def load_experts(t):
            H2 = dram["b1"].shape[1] // E
            if t.n == B + 1:
                sp.dma_start(dram["bo"][:, :], io["bo"].unsqueeze(0).to_broadcast([P, D])
                             ).then_inc(dram["biases_loaded"], 16)
                for e in range(E):
                    sp.dma_start(dram["b1"][:, e * H2:(e + 1) * H2], io["f1_b"][e].unsqueeze(0).to_broadcast([P, H2])
                                 ).then_inc(dram["biases_loaded"], 16)
            if t.n == B + 3:
                wait(sp, "pv_done", 4 * B)
                wait(sp, "exp_done", UNITS * B)
                for e in range(E):
                    sp.dma_start(dram["w1_raw"][:, :, e * H2:(e + 1) * H2],
                                 io["f1_t"][e].rearrange("(c p) h -> p c h", p=P)
                                 ).then_inc(dram["w1_loaded"][e], 16)

        def load_xt(b):
            if active(b):
                wait(sp, "kv_projected", done(b.back(2)))
                sp.dma_start(xt[:, b.s2], io["x_t"][bass.ds(b.n, 1)].rearrange("o (c p) s -> p (o c) s", p=P)
                             ).then_inc(sm[f"xt_loaded{b.s2}"], 16)

        def step(t):
            load_xt(t)
            if t.fixed and t.n == 0:
                load_setup()
            b = t.back(6)
            if active(b):
                wait(sp, "x2_ready", done(b))
                rows = dram["sum"][0:B * S, :].rearrange("(b s) d -> b s d", s=S)[bass.ds(b.n, 1)]
                sp.dma_start(rows.rearrange("o (c p) d -> p (o c) d", p=P), x2[:, b.s2, :, 0:D]
                             ).then_inc(sm[f"x2_stored{b.s2}"], 16)
            b = t.back(3)
            if active(b):
                wait(sp, "y1_ready", done(b.back(2)))
                sp.dma_start(xres[:, b.s2], io["x"][bass.ds(b.n, 1)].rearrange("o (c p) d -> p (o c) d", p=P)
                             ).then_inc(sm[f"xres_loaded{b.s2}"], 16)
            b = t.back(4)
            if active(b):
                wait(sp, "cross_out", done(b.back(2)))
                sp.dma_start(ctxv[:, b.s2], io["context"][bass.ds(b.n, 1)].rearrange("o k d -> (o k) d")
                             ).then_inc(sm[f"ctxv_loaded{b.s2}"], 16)
            b = t.back(2)
            if active(b):
                wait(sp, "m_copied", done(b))
                sp.dma_start(qstack[KROWS:KROWS + MROWS, b.s4], mrows[:, b.s2]).then_inc(sm[f"m_stacked{b.s2}"], 16)
            b = t
            if active(b):
                wait(sp, "q1_cast", done(b))
                wait(sp, "q_split", done(b, 2))
                sp.dma_start(dram["q"][b.s2].rearrange("t (c p) s -> p t c s", p=P), qpart[:, b.s2]
                             ).then_inc(sm["q_stored"], 16)
                wait(sp, "q_stored", done(b, 16))
                wait(sp, "scored", done(b.back(4), UNITS))
                for i, part in enumerate(QPART):
                    sp.dma_start(qstack[i * DK:(i + 1) * DK, b.s4],
                                 dram["q"][b.s2, part].rearrange("(h d) s -> d h s", d=DK)
                                 ).then_inc(sm[f"q_stacked{b.s2}"], 16)
            if t.fixed:
                load_experts(t)

        pipeline(sp, step)
        for s in range(2):
            sp.wait_ge(sm[f"x2_stored{s}"], 16 * (B // 2))

    @block.gpsimd
    def _(pool):
        pool.memset(ident[:, :], 0.0).then_inc(sm["pool_chain"], 1)
        pool.memset(neg_half[:, :], -0.5)
        pool.memset(neg_one[:, :], -1.0)
        pool.memset(eps_c[:, :], EPS)
        pool.memset(all_ones[:, :], 1.0)
        pool.memset(before[:, :], 1.0)
        pool.iota(base[:, 0, :], pattern=[[STRIDE, E]], base=0, channel_multiplier=0,
                  allow_small_or_imprecise_dtypes=True)
        for s in range(2):
            pool.iota(x2[:, s, :, D + E], pattern=[[P, QC]], base=s * S, channel_multiplier=1,
                      allow_small_or_imprecise_dtypes=True)
        pool.memset(one_c[:, :], 1.0)
        pool.memset(ones_row[:, :], 1.0)
        pool.iota(iota_e[:, :, :], pattern=[[0, QC], [1, E]], base=0, channel_multiplier=0,
                  allow_small_or_imprecise_dtypes=True)
        pool.memset(vaug[:, :, :, :], 0.0).then_inc(sm["pool_chain"], 1)
        pool.wait_ge(sm["pool_chain"], 2)
        pool.memset(vaug[:, :, :, DK:DK + 1], 1.0)
        pool.affine_select(out=ident[:, :], in_=ident[:, :], compare_op=ALU.not_equal, fill=1.0, base=0,
                           pattern=[[-1, P]], channel_multiplier=1).then_inc(sm["pool_chain"], 1)
        pool.wait_ge(sm["pool_chain"], 3)
        pool.affine_select(out=before[:, :], in_=before[:, :], compare_op=ALU.is_gt, fill=0.0, base=0,
                           pattern=[[1, P]], channel_multiplier=-1)
        pool.tensor_copy(ident_b[:, :], ident[:, :]).then_inc(sm["consts_made"], 1)

        def rstd(b, var, mv, vare, nmean, out, shift, ready):
            wait(pool, var, done(b))
            pool.tensor_tensor(vare[:, b.s2], mv[:, b.s2, :, 1], eps_c[:, :], ALU.add)
            pool.tensor_tensor(nmean[:, b.s2], mv[:, b.s2, :, 0], neg_one[:, :], ALU.mult).then_inc(sm[ready], 1)
            wait(pool, ready, 3 * b.n + 1)
            pool.tensor_tensor(out[:, b.s2], vare[:, b.s2], neg_half[:, :], ALU.pow).then_inc(sm[ready], 1)
            wait(pool, ready, 3 * b.n + 2)
            pool.tensor_tensor(shift[:, b.s2], nmean[:, b.s2], out[:, b.s2], ALU.mult).then_inc(sm[ready], 1)

        def step(t):
            b7, b6, b4 = t.back(7), t.back(6), t.back(4)
            if active(b6):
                rstd(b6, "var2_ready", mv2, vare2, nmean2, rstd2, shift2, "rstd2_ready")
            if active(t):
                wait(pool, "q_rest", done(t))
                wait(pool, "q_stored", done(t.back(2), 16))
                pool.tensor_tensor(qpart[:, t.s2, 1], qrest[:, t.s2], one_c[:, :].unsqueeze(2).to_broadcast([P, DC, S]),
                                   ALU.mult).then_inc(sm["q_split"], 1)
                wait(pool, "slots_ready", done(b7))
                wait(pool, "q_split", 2 * t.n + 1)
                pool.tensor_tensor(qpart[:, t.s2, 2], qrest[:, t.s2], qpart[:, t.s2, 1], ALU.subtract
                                   ).then_inc(sm["q_split"], 1)
            if active(b7):
                if not active(t):
                    wait(pool, "slots_ready", done(b7))
                for c in range(QC):
                    for k in range(2):
                        pool.indirect_dma_start(
                            out=dram["lists"], out_offset=bass.IndirectOffsetOnAxis(
                                ap=slots[:, b7.s2, 2 * c + k:2 * c + k + 1], axis=0),
                            in_=x2[:, b7.s2, c, :], in_offset=None).then_inc(sm[f"dispatched{b7.s2}"], 16)
            if active(b4):
                wait(pool, "att_normed", done(b4, 2))
                wait(pool, f"xres_loaded{b4.s2}", 16 * b4.half + 16)
                pool.tensor_tensor(y1[:, b4.s2], att[:, b4.s2], xres[:, b4.s2], ALU.add).then_inc(sm["y1_ready"], 1)
                rstd(b4, "var1_ready", mv1, vare1, nmean1, rstd1, shift1, "rstd1_ready")

        pipeline(pool, step)
        for s in range(2):
            pool.wait_ge(sm[f"dispatched{s}"], 2 * QC * 16 * (B // 2))

    @block.tensor
    def _(pe):
        mm = nc.tensor.matmul
        pe.wait_ge(sm["projections_loaded"], 16 * (2 + KROWS // DK))
        pe.wait_ge(sm["consts_made"], 1)

        def fold_projections():
            pe.wait_ge(sm["setup_loaded"], 16 * 6)
            for oc in range(DC):
                for k in range(DC):
                    last = mm(psO[:, oc, 0:D], w2t[:, k, oc * P:(oc + 1) * P], w1[:, k, :], start=k == 0,
                              stop=k == DC - 1)
            last.then_inc(sm["wc_product"], 1)
            for oc in range(DC):
                for k in range(DC):
                    last = mm(psT[:, 0, oc:oc + 1], w2t[:, k, oc * P:(oc + 1) * P], b1c[:, k:k + 1], start=k == 0,
                              stop=k == DC - 1)
            last.then_inc(sm["c_product"], 1)
            pe.wait_ge(sm["wc_copied"], 2)
            for ic in range(DC):
                for k in range(DC):
                    mm(psO[:, ic, 0:D], wc[:, k, ic * P:(ic + 1) * P], wc[:, k, :], start=k == 0, stop=k == DC - 1)
            for ic in range(DC):
                for k in range(DC):
                    mm(psT[:, 1, ic:ic + 1], wc[:, k, ic * P:(ic + 1) * P], cvec[:, k:k + 1], start=k == 0,
                       stop=k == DC - 1)
            for k in range(DC):
                last = mm(psA[0:1, 0:1], cvec[:, k:k + 1], cvec[:, k:k + 1], start=k == 0, stop=k == DC - 1)
            last.then_inc(sm["gram_product"], 1)
            pe.wait_ge(sm["gram_copied"], 2)

        def map_contexts(g):
            pe.wait_ge(sm["ctx_group_odd" if g % 2 else "ctx_group_even"], 16 * (g // 2 + 1))
            if g >= 1:
                pe.wait_ge(sm["keymap_copied"], 3 * g)
            for ic in range(DC):
                for k in range(DC):
                    mm(psO[:, ic, 0:GROUP], gram[:, k, ic * P:(ic + 1) * P], ctx_t[:, k, g % 2, :],
                       start=k == 0, stop=k == DC - 1)
            for k in range(DC):
                last = mm(psT[0:1, 0, 0:GROUP], uvec[:, k:k + 1], ctx_t[:, k, g % 2, :], start=k == 0,
                          stop=k == DC - 1)
            last.then_inc(sm["keymap_product"], 1)

        bank_a = {"x1_transposed": ("x1t_copied", 5, 1, 1), "cross_scored": ("score_link", 5, 1, 1),
                  "m_transposed": ("m_copied", 2, 1, 1), "att_transposed0": ("att_normed", 4, 2, 1),
                  "att_transposed1": ("att_normed", 4, 2, 2), "cross_out": ("y2_ready", 5, 1, 1)}
        bank_b = {"q_projected": ("q_rest", 0, 1, 1), "x2_transposed": ("x2t_copied", 6, 1, 1),
                  "gate_scored": ("gate_link", 6, 7, 1), "cprob_transposed": ("cprobt_copied", 5, 1, 1),
                  "kv_projected": ("k_rest", 0, 1, 1), "counted": ("slot_link", 6, 3, 1)}

        def bank_read(bank, t, use):
            order = list(bank)
            i = order.index(use)
            for k in range(len(order)) if t.fixed else ((i - 1) % len(order),):
                name, lag, per, nth = bank[order[k]]
                b = t.back(lag + (k >= i))
                if b.fixed:
                    b = clamp(b)
                wait(pe, name, per * b.n + nth)

        def att_transpose(t, g):
            b = t.back(4)
            wait(pe, "att_copied", 2 * b.n + g + 1)
            bank_read(bank_a, t, f"att_transposed{g}")
            for c in range(QC):
                for hh in range(2):
                    last = nc.tensor.transpose(psA[:, (c * 2 + hh) * P:(c * 2 + hh + 1) * P],
                                               att_t[:, g, hh * S + c * P:hh * S + (c + 1) * P], ident[:, :])
            last.then_inc(sm["att_transposed"], 1)

        def pv(b, w):
            g, kc = w // 2, w % 2
            wait(pe, "exp_done", UNITS * b.n + 4 * w + 4)
            if kc == 0:
                wait(pe, "att_copied", 2 * b.n + g - 1)
            for i in range(4):
                last = mm(psO[32 * i:32 * i + 32, g, :], vaug[:, b.s4, kc, :], probs[:, (4 * w + i) % PT, :],
                          start=kc == 0, stop=kc == 1)
            last.then_inc(sm["pv_done"], 1)

        def step(t):
            b1, b2, b3, b4, b5, b6 = (t.back(k) for k in range(1, 7))
            for u in range(UNITS):
                for g in context_group(t, u):
                    map_contexts(g)
                if u == 1 and active(b4):
                    pv(b4, 3)
                if u == 1 and active(b5):
                    wait(pe, "x1_ready", done(b5))
                    bank_read(bank_a, t, "x1_transposed")
                    for c in range(QC):
                        for k in range(DC):
                            last = nc.tensor.transpose(psA[:, k * S + c * P:k * S + (c + 1) * P],
                                                       x1[:, b5.s2, c, k * P:(k + 1) * P], ident[:, :])
                    last.then_inc(sm["x1_transposed"], 1)
                if u == 2 and active(t):
                    wait(pe, f"xt_loaded{t.s2}", 16 * t.half + 16)
                    bank_read(bank_b, t, "q_projected")
                    for oc in range(DC):
                        for k in range(DC):
                            last = mm(psB[:, oc * S:(oc + 1) * S], wq[:, k, oc * P:(oc + 1) * P], xt[:, t.s2, k, :],
                                      start=k == 0, stop=k == DC - 1)
                    last.then_inc(sm["q_projected"], 1)
                if u == 4 and active(b5):
                    wait(pe, "x1t_copied", done(b5))
                    bank_read(bank_a, t, "cross_scored")
                    for c in range(QC):
                        for k in range(DC):
                            mm(psA[:, c * SC:(c + 1) * SC], x1t[:, b5.s2, k, c * P:(c + 1) * P],
                               keymap[:, k, bass.ds(b5.n * SC, SC)], start=k == 0, stop=False)
                        last = mm(psA[:, c * SC:(c + 1) * SC], ones_row[:, :], keybias[:, bass.ds(b5.n * SC, SC)],
                                  start=False, stop=True)
                    last.then_inc(sm["cross_scored"], 1)
                if u == 5 and active(b6):
                    wait(pe, "x2_ready", done(b6))
                    bank_read(bank_b, t, "x2_transposed")
                    for c in range(QC):
                        for k in range(DC):
                            last = nc.tensor.transpose(psB[:, k * S + c * P:k * S + (c + 1) * P],
                                                       x2[:, b6.s2, c, k * P:(k + 1) * P], ident[:, :])
                    last.then_inc(sm["x2_transposed"], 1)
                if u == 6 and active(b2):
                    wait(pe, "m_split", done(b2))
                    bank_read(bank_a, t, "m_transposed")
                    nc.tensor.transpose(psA[0:MROWS * NH * QC, 0:P // 2].bitcast(BF16),
                                        mpart[:, b2.s2].rearrange("p m h c -> p (m h c)"), ident_b[:, :]
                                        ).then_inc(sm["m_transposed"], 1)
                if u == 7 and active(b6):
                    wait(pe, "x2t_copied", done(b6))
                    bank_read(bank_b, t, "gate_scored")
                    for c in range(QC):
                        for k in range(DC):
                            last = mm(psB[:, c * E:(c + 1) * E], x2t[:, b6.s2, k, c * P:(c + 1) * P], wg[:, k, :],
                                      start=k == 0, stop=k == DC - 1)
                    last.then_inc(sm["gate_scored"], 1)
                if u == 8 and active(b4):
                    att_transpose(t, 0)
                if u == 10 and active(b4):
                    att_transpose(t, 1)
                if u == 9 and active(b5):
                    wait(pe, "cross_exp", done(b5))
                    bank_read(bank_b, t, "cprob_transposed")
                    for c in range(QC):
                        last = nc.tensor.transpose(psB[0:SC, c * P:(c + 1) * P], cprob[:, b5.s2, c, :], ident[:, :])
                    last.then_inc(sm["cprob_transposed"], 1)
                if u == 11 and active(t):
                    bank_read(bank_b, t, "kv_projected")
                    for k in range(DC):
                        mm(psB[0:KROWS, 0:S], wk[:, k, :], xt[:, t.s2, k, :], start=k == 0, stop=k == DC - 1)
                    for c in range(QC):
                        for k in range(DC):
                            last = mm(psB[:, S + c * DK:S + (c + 1) * DK], xt[:, t.s2, k, c * P:(c + 1) * P],
                                      wv[:, k, :], start=k == 0, stop=k == DC - 1)
                    last.then_inc(sm["kv_projected"], 1)
                if u == 14 and active(b5):
                    wait(pe, "cprobt_copied", done(b5))
                    wait(pe, f"ctxv_loaded{b5.s2}", 16 * b5.half + 16)
                    bank_read(bank_a, t, "cross_out")
                    for c in range(QC):
                        last = mm(psA[:, c * D:(c + 1) * D], cprob_t[:, b5.s2, c * P:(c + 1) * P], ctxv[:, b5.s2, :],
                                  start=True, stop=True)
                    last.then_inc(sm["cross_out"], 1)
                if u == 15 and active(b6):
                    wait(pe, "hot_ready", done(b6))
                    bank_read(bank_b, t, "counted")
                    h0, h1 = hotsum[:, b6.s2, 0, :], hotsum[:, b6.s2, 1, :]
                    mm(psB[:, 0:E], before[:, :], h0, start=True, stop=True)
                    mm(psB[:, E:2 * E], before[:, :], h1, start=True, stop=False)
                    mm(psB[:, E:2 * E], all_ones[:, :], h0, start=False, stop=True)
                    mm(psB[:, 2 * E:3 * E], all_ones[:, :], h0, start=True, stop=False)
                    mm(psB[:, 2 * E:3 * E], all_ones[:, :], h1, start=False, stop=True
                       ).then_inc(sm["counted"], 1)
                if active(b1):
                    if u == 0:
                        wait(pe, f"q_stacked{b1.s2}", 6 * 16 * (b1.half + 1))
                        wait(pe, "k_split", done(b1))
                    wait(pe, "max_reduced", UNITS * b1.n + u - 1)
                    c, hp = u // 8, u % 8
                    for hh in range(2):
                        last = mm(psS[:, u % 2, hh * S:(hh + 1) * S],
                                  qstack[0:KROWS, b1.s4, 2 * hp + hh, c * P:(c + 1) * P], kstack[0:KROWS, b1.s4, :],
                                  start=True, stop=True)
                    last.then_inc(sm["max_scored"], 1)
                if active(b3):
                    if u == 0:
                        wait(pe, f"m_stacked{b3.s2}", 16 * b3.half + 16)
                    g, kc, i = u // 8, u // 4 % 2, u % 4
                    wait(pe, "exp_done", UNITS * b3.n + u - 1)
                    heads = qstack[0:KROWS + MROWS, b3.s4, 8 * g + i:8 * g + i + 5:4, :]
                    mm(psT[:, u % 2, :], kstack[0:KROWS + MROWS, b3.s4, kc * P:(kc + 1) * P], heads,
                       start=True, stop=True).then_inc(sm["scored"], 1)
                    if u % 4 == 1 and u > 4:
                        pv(b3, u // 4 - 1)
            if t.fixed and t.n == 0:
                fold_projections()
            for g in context_group(t, UNITS):
                map_contexts(g)
            if t.fixed and t.n == 2:
                wait(pe, "keymap_copied", 3 * NGROUP)

        pipeline(pe, step)

    @block.scalar
    def _(act):
        copy = nc.scalar.copy
        act.wait_ge(sm["consts_made"], 1)

        def copy_projections():
            act.wait_ge(sm["wc_product"], 1)
            for oc in range(DC):
                last = copy(wc[:, oc, :], psO[:, oc, 0:D])
            last.then_inc(sm["wc_copied"], 1)
            act.wait_ge(sm["gram_product"], 1)
            for ic in range(DC):
                last = copy(gram[:, ic, :], psO[:, ic, 0:D])
            last.then_inc(sm["gram_copied"], 1)
            act.wait_ge(sm["gram_copied"], 2)

        def copy_keymap(g):
            act.wait_ge(sm["keymap_product"], g + 1)
            for ic in range(DC):
                nc.scalar.activation(keymap[:, ic, g * GROUP:(g + 1) * GROUP], psO[:, ic, 0:GROUP], ACT.Identity,
                                     bias=uvec[:, ic:ic + 1]).then_inc(sm["keymap_copied"], 1)
            if g + 2 < NGROUP:
                load_context_group(act, g + 2)

        def norm(x, rs, shift, y, b, ready, name):
            wait(act, ready, done(b, 3))
            for c in range(QC):
                last = nc.scalar.activation(x[:, b.s2, c, 0:D], y[:, b.s2, c, :], ACT.Identity,
                                            scale=rs[:, b.s2, c:c + 1], bias=shift[:, b.s2, c:c + 1])
            last.then_inc(sm[name], 1)

        def copy_att(b, g):
            wait(act, "pv_done", 4 * b.n + 2 * g + 2)
            wait(act, "att_transposed", 2 * b.n + g - 1)
            copy(att_t[:, g, :], psO[:, g, :]).then_inc(sm["att_copied"], 1)

        def step(t):
            b2, b3, b4, b5, b6 = (t.back(k) for k in range(2, 7))
            for u in range(UNITS):
                for g in context_group(t, u):
                    copy_keymap(g)
                if u == 0 and active(b5):
                    wait(act, "y2_ready", done(b5.back(2)))
                    wait(act, "x1_transposed", done(b5.back(2)))
                    norm(x1, rstd1, shift1, y1, b5, "rstd1_ready", "x1_ready")
                if u == 2 and active(b4):
                    copy_att(b4, 1)
                if u == 2 and active(b5):
                    wait(act, "x1_transposed", done(b5))
                    wait(act, "cross_scored", done(b5.back(2)))
                    copy(x1t[:, b5.s2].rearrange("p c s -> p (c s)"), psA[:, :]).then_inc(sm["x1t_copied"], 1)
                if u == 3 and active(t):
                    wait(act, "q_projected", done(t))
                    wait(act, "q_stored", done(t.back(2), 16))
                    copy(qpart[:, t.s2, 0].rearrange("p c s -> p (c s)"), psB[:, :]).then_inc(sm["q1_cast"], 1)
                if u == 4 and active(b6):
                    wait(act, f"x2_stored{b6.s2}", 16 * b6.half)
                    wait(act, "x2_transposed", done(b6.back(2)))
                    wait(act, f"dispatched{b6.s2}", 2 * QC * 16 * b6.half)
                    norm(x2, rstd2, shift2, y2, b6, "rstd2_ready", "x2_ready")
                if u == 6 and active(b6):
                    wait(act, "x2_transposed", done(b6))
                    wait(act, "gate_scored", done(b6.back(2)))
                    copy(x2t[:, b6.s2].rearrange("p c s -> p (c s)"), psB[:, :]).then_inc(sm["x2t_copied"], 1)
                if u == 7 and active(b2):
                    wait(act, "m_transposed", done(b2))
                    wait(act, f"m_stacked{b2.s2}", 16 * b2.half)
                    copy(mrows[:, b2.s2], psA[0:MROWS * NH * QC, 0:P // 2].bitcast(BF16)).then_inc(sm["m_copied"], 1)
                if u == 7 and active(b5):
                    wait(act, "cross_masked", done(b5))
                    wait(act, "cprob_transposed", done(b5.back(2)))
                    wait(act, "y2_ready", done(b5.back(2)))
                    for c in range(QC):
                        last = nc.scalar.activation(cprob[:, b5.s2, c, :], cscore[:, b5.s2, c, :], ACT.Exp,
                                                    bias=cnegmax[:, b5.s2, c:c + 1],
                                                    accum_out=csum[:, b5.s2, c:c + 1])
                    last.then_inc(sm["cross_exp"], 1)
                if u == 10 and active(b5):
                    wait(act, "cprob_transposed", done(b5))
                    wait(act, "cross_out", done(b5.back(2)))
                    copy(cprob_t[:, b5.s2], psB[0:SC, 0:S]).then_inc(sm["cprobt_copied"], 1)
                if u == 11 and active(b6):
                    wait(act, "gate_max", done(b6))
                    wait(act, "comb_ready", done(b6.back(2)))
                    for c in range(QC):
                        nc.scalar.activation(gexp[:, b6.s2, c, :], logits[:, b6.s2, c, :], ACT.Exp,
                                             bias=gneg[:, b6.s2, c:c + 1], accum_out=gsum[:, b6.s2, c:c + 1])
                        last = nc.scalar.activation(gtop[:, b6.s2, c, :], top[:, b6.s2, c, 0:2], ACT.Exp,
                                                    bias=gneg[:, b6.s2, c:c + 1])
                    last.then_inc(sm["gate_exp"], 1)
                if u == 12 and active(t):
                    wait(act, "kv_projected", done(t))
                    wait(act, "pv_done", 4 * (t.n - 3))
                    wait(act, "scored", UNITS * (t.n - 3))
                    copy(vaug[:, t.s4, :, 0:DK], psB[:, S:S + QC * DK].rearrange("p (c d) -> p c d", c=QC))
                    copy(kstack[0:KROWS, t.s4], psB[0:KROWS, 0:S]).then_inc(sm["kv_cast"], 1)
                if u == 13 and active(t):
                    wait(act, "k_rest", done(t))
                    copy(kstack[32:64, t.s4], krest[32:64, t.s2])
                    copy(ksmall[64:80, t.s2], krest[64:80, t.s2]).then_inc(sm["k_mid"], 1)
                if active(b3):
                    wait(act, "scored", UNITS * b3.n + u + 1)
                    if u % 4 == 0:
                        wait(act, "pv_done", 4 * b3.n + u // 4 - 1)
                    nc.scalar.activation(probs[:, u % PT, :], psT[:, u % 2, :], ACT.Exp, scale=SELF_SCALE
                                         ).then_inc(sm["exp_done"], 1)
                    if u == 11:
                        copy_att(b3, 0)
            if t.fixed and t.n == 0:
                copy_projections()
            for g in context_group(t, UNITS):
                copy_keymap(g)

        pipeline(act, step)

    @block.vector
    def _(dve):
        v = nc.vector
        v.memset(kstack[KROWS:KROWS + MROWS], 1.0)
        dve.wait_ge(sm["consts_made"], 1)

        def copy_vectors():
            dve.wait_ge(sm["setup_loaded"], 16 * 6)
            dve.wait_ge(sm["c_product"], 1)
            v.tensor_tensor(cvec[:, :], psT[:, 0, 0:DC], b2c[:, :], ALU.add).then_inc(sm["wc_copied"], 1)
            dve.wait_ge(sm["gram_product"], 1)
            v.tensor_copy(uvec[:, :], psT[:, 1, 0:DC])
            v.tensor_copy(c_dot_c[:, :], psA[0:1, 0:1]).then_inc(sm["gram_copied"], 1)
            dve.wait_ge(sm["gram_copied"], 2)

        def copy_keybias(g):
            dve.wait_ge(sm["keymap_product"], g + 1)
            v.tensor_scalar(keybias[:, g * GROUP:(g + 1) * GROUP], psT[0:1, 0, 0:GROUP], c_dot_c[:, :], None, ALU.add
                            ).then_inc(sm["keymap_copied"], 1)

        def stats(y, out, b, name):
            for c in range(QC):
                last = v.bn_stats(out[:, b.s2, c, :], y[:, b.s2, c, :])
            last.then_inc(sm[name], 1)

        def moments(out, mv, b, name):
            for c in range(QC):
                last = v.bn_aggr(mv[:, b.s2, c, :], out[:, b.s2, c, :])
            last.then_inc(sm[name], 1)

        def att_view(b, g):
            return psA[:, :].rearrange("p (c j k) -> p c j k", c=QC, k=32), rden[:, g].rearrange("p (c j) -> p c j", c=QC)

        def att_reciprocal(b, g):
            view, rec = att_view(b, g)
            wait(dve, "att_transposed", 2 * b.n + g + 1)
            v.reciprocal(rec, view[:, :, :, DK]).then_inc(sm["den_ready"], 1)

        def att_norm(b, g):
            view, rec = att_view(b, g)
            wait(dve, "y1_ready", done(b.back(2)))
            wait(dve, "den_ready", 2 * b.n + g + 1)
            v.tensor_tensor(att[:, b.s2, :, g * P:(g + 1) * P].rearrange("p c (j k) -> p c j k", k=DK),
                            view[:, :, :, 0:DK], rec.unsqueeze(3).to_broadcast([P, QC, 8, DK]), ALU.mult
                            ).then_inc(sm["att_normed"], 1)

        def split_max(b, k):
            m, r, part = negmax[:, b.s2], mrest[:, b.s2], mpart[:, b.s2]
            if k == 0:
                wait(dve, "max_reduced", UNITS * (b.n + 1))
                wait(dve, "m_transposed", done(b.back(2)))
                v.tensor_copy(part[:, 0], m).then_inc(sm["m_link"], 1)
                return
            wait(dve, "m_link", 3 * b.n + k)
            if k == 1:
                v.tensor_tensor(r, m, part[:, 0], ALU.subtract).then_inc(sm["m_link"], 1)
            elif k == 2:
                v.tensor_copy(part[:, 1], r).then_inc(sm["m_link"], 1)
            else:
                v.tensor_tensor(part[:, 2], r, part[:, 1], ALU.subtract).then_inc(sm["m_split"], 1)

        def step(t):
            b1, b2, b4, b5, b6, b7 = (t.back(k) for k in (1, 2, 4, 5, 6, 7))
            gate = lambda k: dve.wait_ge(sm["gate_link"], done(b6, 7, k))
            for u in range(UNITS):
                for g in context_group(t, u):
                    copy_keybias(g)
                if u == 1 and active(b6):
                    wait(dve, "stats2_ready", done(b6))
                if u == 9 and active(b6):
                    wait(dve, "gate_max", done(b6))
                if u == 13 and active(b4):
                    wait(dve, "stats1_ready", done(b4))
                if active(b1):
                    wait(dve, "max_scored", UNITS * b1.n + u + 1)
                    c, hp = u // 8, u % 8
                    v.tensor_reduce(negmax[:, b1.s2, 2 * hp:2 * hp + 2, c],
                                    psS[:, u % 2, :].rearrange("p (h k) -> p h k", h=2), AX.X, ALU.max, negate=True
                                    ).then_inc(sm["max_reduced"], 1)
                if u == 0 and active(b6):
                    wait(dve, "y2_ready", done(b6))
                    stats(y2, stats2, b6, "stats2_ready")
                if u == 0 and active(b7):
                    wait(dve, "slot_link", 3 * b7.n + 1)
                    v.tensor_tensor(chosen[:, b7.s2], hot[:, b7.s2],
                                    place[:, b7.s2].unsqueeze(2).to_broadcast([P, QC, 2, E]), ALU.mult
                                    ).then_inc(sm["slot_link"], 1)
                if u == 1 and active(b6):
                    moments(stats2, mv2, b6, "var2_ready")
                if u == 1 and active(b7):
                    wait(dve, "slot_link", 3 * b7.n + 2)
                    v.tensor_reduce(slotf[:, b7.s2], chosen[:, b7.s2], AX.X, ALU.add).then_inc(sm["slot_link"], 1)
                if 1 <= u <= 4 and active(b2):
                    split_max(b2, u - 1)
                if u == 2 and active(b7):
                    wait(dve, "slot_link", 3 * b7.n + 3)
                    v.tensor_copy(slots[:, b7.s2], slotf[:, b7.s2].rearrange("p c k -> p (c k)")
                                  ).then_inc(sm["slots_ready"], 1)
                if u == 3 and active(t):
                    wait(dve, "q1_cast", done(t))
                    wait(dve, "q_split", done(t.back(2), 2))
                    v.tensor_tensor(qrest[:, t.s2].rearrange("p c s -> p (c s)"), psB[:, :],
                                    qpart[:, t.s2, 0].rearrange("p c s -> p (c s)"), ALU.subtract
                                    ).then_inc(sm["q_rest"], 1)
                if u == 4 and active(b5):
                    wait(dve, "cross_scored", done(b5))
                    wait(dve, "cross_exp", done(b5.back(2)))
                    v.scalar_tensor_tensor(cscore[:, b5.s2], psA[:, 0:QC * SC].rearrange("p (c k) -> p c k", c=QC),
                                           CROSS_SCALE, mask[:, :, :], ALU.mult, ALU.add).then_inc(sm["score_link"], 1)
                if u == 5 and active(b5):
                    wait(dve, "score_link", done(b5))
                    v.tensor_reduce(cnegmax[:, b5.s2], cscore[:, b5.s2], AX.X, ALU.max, negate=True
                                    ).then_inc(sm["cross_masked"], 1)
                if u == 7 and active(b6):
                    wait(dve, "gate_scored", done(b6))
                    wait(dve, "gate_exp", done(b6.back(2)))
                    v.tensor_copy(logits[:, b6.s2], psB[:, 0:QC * E].rearrange("p (c e) -> p c e", c=QC)
                                  ).then_inc(sm["gate_link"], 1)
                if u == 8 and active(b4):
                    att_reciprocal(b4, 0)
                if u == 8 and active(b6):
                    gate(1)
                    v.tensor_reduce(gneg[:, b6.s2], logits[:, b6.s2], AX.X, ALU.max, negate=True)
                    for c in range(QC):
                        last = v.max(top[:, b6.s2, c, :], logits[:, b6.s2, c, :])
                    last.then_inc(sm["gate_max"], 1)
                if u == 8 and active(b4):
                    att_norm(b4, 0)
                if u == 9 and active(b6):
                    for c in range(QC):
                        last = v.max_index(topi[:, b6.s2, c, :], top[:, b6.s2, c, :], logits[:, b6.s2, c, :])
                    last.then_inc(sm["gate_link"], 1)
                if u == 10 and active(b4):
                    att_reciprocal(b4, 1)
                if u == 10 and active(b6):
                    gate(2)
                    v.tensor_copy(topf[:, b6.s2], topi[:, b6.s2, :, 0:2]).then_inc(sm["gate_link"], 1)
                if u == 10 and active(b4):
                    att_norm(b4, 1)
                if u == 10 and active(b6):
                    gate(3)
                    v.tensor_tensor(hot[:, b6.s2], iota_e[:, :, :].unsqueeze(2).to_broadcast([P, QC, 2, E]),
                                    topf[:, b6.s2].unsqueeze(3).to_broadcast([P, QC, 2, E]), ALU.is_equal
                                    ).then_inc(sm["gate_link"], 1)
                if u == 11 and active(b6):
                    gate(4)
                    wait(dve, "counted", done(b6.back(2)))
                    v.tensor_tensor(hotsum[:, b6.s2], hot[:, b6.s2, :, 0, :], hot[:, b6.s2, :, 1, :], ALU.add
                                    ).then_inc(sm["hot_ready"], 1)
                if u == 12 and active(t):
                    wait(dve, "kv_cast", done(t))
                    wait(dve, "k_split", done(t.back(2)))
                    v.tensor_tensor(krest[0:KROWS, t.s2], psB[0:KROWS, 0:S], kstack[0:KROWS, t.s4], ALU.subtract
                                    ).then_inc(sm["k_rest"], 1)
                if u == 12 and active(b4):
                    wait(dve, "y1_ready", done(b4))
                    stats(y1, stats1, b4, "stats1_ready")
                if u == 12 and active(b6):
                    wait(dve, "gate_exp", done(b6))
                    v.scalar_tensor_tensor(gden[:, b6.s2], gsum[:, b6.s2], GATE_EPS, gtop[:, b6.s2, :, 0], ALU.mult,
                                           ALU.add).then_inc(sm["gate_link"], 1)
                if u == 13 and active(b4):
                    moments(stats1, mv1, b4, "var1_ready")
                if u == 13 and active(b6):
                    gate(5)
                    v.tensor_tensor(gden[:, b6.s2], gden[:, b6.s2], gtop[:, b6.s2, :, 1], ALU.add
                                    ).then_inc(sm["gate_link"], 1)
                if u == 14 and active(t):
                    wait(dve, "k_mid", done(t))
                    v.tensor_tensor(kstack[64:80, t.s4], krest[64:80, t.s2], ksmall[64:80, t.s2], ALU.subtract
                                    ).then_inc(sm["k_split"], 1)
                if u == 13 and active(b5):
                    wait(dve, "cross_exp", done(b5))
                    v.reciprocal(crec[:, b5.s2], csum[:, b5.s2]).then_inc(sm["crec_ready"], 1)
                if u == 14 and active(b6):
                    gate(6)
                    v.reciprocal(gden[:, b6.s2], gden[:, b6.s2]).then_inc(sm["gate_link"], 1)
                if u == 14 and active(b5):
                    wait(dve, "crec_ready", done(b5))
                    wait(dve, "cross_out", done(b5))
                    for c in range(QC):
                        last = v.scalar_tensor_tensor(y2[:, b5.s2, c, :], psA[:, c * D:(c + 1) * D],
                                                      crec[:, b5.s2, c:c + 1], x1[:, b5.s2, c, :], ALU.mult, ALU.add)
                    last.then_inc(sm["y2_ready"], 1)
            if t.fixed and t.n == 0:
                copy_vectors()
            for g in context_group(t, UNITS):
                copy_keybias(g)
            if active(b6):
                gate(7)
                wait(dve, "hot_ready", done(b6))
                for c in range(QC):
                    last = v.scalar_tensor_tensor(x2[:, b6.s2, c, D:D + E], gexp[:, b6.s2, c, :],
                                                  gden[:, b6.s2, c:c + 1], hotsum[:, b6.s2, c, :], ALU.mult, ALU.mult)
                last.then_inc(sm["comb_ready"], 1)
                if not b6.fixed or b6.n >= 2:
                    v.tensor_scalar(x2[:, b6.s2, :, D + E], x2[:, b6.s2, :, D + E], float(2 * S), None, ALU.add)
                wait(dve, "counted", done(b6))
                wait(dve, "slot_link", 3 * b6.n - 2)
                count = psB[:, 0:3 * E].rearrange("p (c e) -> p c e", e=E)
                now, then = base[:, b6.s2, :], base[:, 1 - b6.s2, :]
                v.tensor_tensor(place[:, b6.s2], count[:, 0:QC, :], now.unsqueeze(1).to_broadcast([P, QC, E]), ALU.add)
                v.tensor_tensor(then, count[:, QC, :], now, ALU.add).then_inc(sm["slot_link"], 1)

        pipeline(dve, step)


def experts(nc, ctx, io, dram):
    base = dram["base"]
    T, D = dram["sum"].shape
    T -= P
    E, _, H2 = io["f1_t"].shape
    H = H2 // 2
    DC, HC = D // P, H // P
    ROW = D + E + 1
    STRIDE = dram["stride"]
    TILES = 2 * T // P + E

    def sb(name, shape, dt=F32):
        return ctx.enter_context(nc.sbuf_tensor(name, shape, dt))

    def ps(name, shape, dt=F32):
        return ctx.enter_context(nc.psum_tensor(name, shape, dt))

    I32 = mybir.dt.int32
    w1_lo = sb("w1_lo", [P, DC, E * H2], F32R)
    ident = sb("ident2", [P, P])
    w1_hi = sb("w1_hi", [P, DC, E * H2], F32R)
    w1_raw, b1, bo = dram["w1_raw"], dram["b1"], dram["bo"]
    wo_hi = sb("wo_hi", [P, HC, D], F32R)
    wo_lo = sb("wo_lo", [P, HC, D], F32R)
    cnt = sb("cnt", [P, E])
    cnti = sb("cnti", [P, E], I32)
    ntile = sb("ntile", [P, E])
    upto = sb("upto", [P, E])
    skip = sb("skip", [P, E])
    listbase = sb("listbase", [P, E])
    number = sb("number", [P, TILES])
    past = sb("past", [P, TILES])
    rowf = sb("rowf", [P, TILES])
    expf = sb("expf", [P, TILES])
    row_tab = sb("row_tab", [P, TILES], I32)
    exp_tab = sb("exp_tab", [P, TILES], I32)
    pad_place = sb("pad_place", [P, E])
    pad_rows = sb("pad_rows", [P, E], U32)
    pad = sb("pad", [P, ROW])
    partition = sb("partition", [P, 1])
    with nc.sbuf_tensor("wo_raw", [P, HC, D], F32) as wo_raw:
        pass
    xe = sb("xe", [P, 4, ROW])
    hb = sb("hb", [P, 2, H])
    g = sb("g", [P, 2, H])
    sig = sb("sig", [P, 2, H])
    yb = sb("yb", [P, 2, D])
    y = sb("y", [P, 2, D])
    xet_hi = sb("xet_hi", [P, 2, DC * P], F32R)
    xet_lo = sb("xet_lo", [P, 2, DC * P], F32R)
    gt_hi = sb("gt_hi", [P, 2, HC * P], F32R)
    gt_lo = sb("gt_lo", [P, 2, HC * P], F32R)
    weight = sb("weight", [P, 4, 1])
    token = sb("token", [P, 4], U32)

    psX = ps("psX", [P, 512])
    psG = ps("psG", [P, 512])
    psHa = ps("psHa", [P, 2, 512])
    psHb = ps("psHb", [P, 2, 512])
    psY = ps("psY", [P, 2, 512])

    names = ["wo_loaded", "w1_split_pool", "consts_made2", "pads_written", "table_link", "tables_ready", "pad_rows_ready",
             "xe_loaded0", "xe_loaded1", "xe_loaded2", "xe_loaded3",
             "x_transposed", "b_product", "a_product", "g_transposed", "y_product",
             "w1_rounded", "w1_split", "wo_rounded", "wo_split",
             "xet_rounded", "xet_split", "sig_ready", "gt_rounded", "gt_split",
             "hb_ready", "ha_ready", "g_ready", "yb_ready", "y_ready", "token_ready", "summed"]
    sm = {n: ctx.enter_context(nc.semaphore(n)) for n in names}

    def wait(eng, name, value):
        if isinstance(value, int) and value <= 0:
            return
        eng.wait_ge(sm[name], value)

    def done(i, per=1):
        return per * (i.n + 1)

    def active(i):
        return not i.fixed or 0 <= i.n < TILES

    def pipeline(eng, step):
        for r in range(8):
            step(Step(0, r))
        with eng.Fori(2, TILES // 4) as j:
            for r in range(4):
                step(Step(j, r))
        for r in range(4):
            step(Step(TILES // 4, r))

    POOL_SPLITS = (1, 4, 6)

    def split_w1(ops, eng, e, name):
        part = slice(e * H2, (e + 1) * H2)
        eng.wait_ge(sm["w1_rounded"], e + 1)
        ops.tensor_tensor(w1_lo[:, :, part], w1_raw[:, :, part], w1_hi[:, :, part].bitcast(F32), ALU.subtract
                          ).then_inc(sm[name], 1)

    block = ctx.enter_context(nc.Block())

    @block.sync
    def _(sp):
        sp.dma_start(wo_raw[:, :, :], io["wo_t"].rearrange("(c p) d -> p c d", p=P)).then_inc(sm["wo_loaded"], 16)
        sp.wait_ge(sm["wo_split"], 1)
        sp.wait_ge(sm["tables_ready"], 2)
        sp.wait_ge(sm["pads_written"], 16 * (E + 2))

        def step(t):
            if active(t):
                wait(sp, "y_ready", done(t.back(4)))
                row = sp.value_load(row_tab[0:1, bass.ds(t.n, 1)], min_val=0, max_val=E * STRIDE)
                sp.dma_start(xe[:, t.s4], dram["lists"][bass.ds(row, P), :]).then_inc(sm[f"xe_loaded{t.s4}"], 16)

        pipeline(sp, step)

    @block.gpsimd
    def _(pool):
        pool.memset(ident[:, :], 0.0)
        pool.memset(pad[:, :], 0.0).then_inc(sm["consts_made2"], 1)
        pool.iota(partition[:, :], pattern=[[0, 1]], base=0, channel_multiplier=1, allow_small_or_imprecise_dtypes=True)
        pool.iota(listbase[:, :], pattern=[[STRIDE, E]], base=0, channel_multiplier=0,
                  allow_small_or_imprecise_dtypes=True)
        pool.iota(number[:, :], pattern=[[1, TILES]], base=0, channel_multiplier=0, allow_small_or_imprecise_dtypes=True)
        pool.wait_ge(sm["consts_made2"], 1)
        pool.affine_select(out=ident[:, :], in_=ident[:, :], compare_op=ALU.not_equal, fill=1.0, base=0,
                           pattern=[[-1, P]], channel_multiplier=1)
        pool.iota(pad[:, ROW - 1:ROW], pattern=[[0, 1]], base=T, channel_multiplier=1,
                  allow_small_or_imprecise_dtypes=True).then_inc(sm["consts_made2"], 1)
        pool.wait_ge(sm["consts_made2"], 2)
        pool.dma_start(dram["lists"][E * STRIDE:E * STRIDE + P, :], pad[:, :]).then_inc(sm["pads_written"], 16)
        pool.dma_start(dram["sum"][T:T + P, :], pad[:, 0:D]).then_inc(sm["pads_written"], 16)
        pool.wait_ge(sm["pad_rows_ready"], 1)
        for e in range(E):
            pool.indirect_dma_start(out=dram["lists"], out_offset=bass.IndirectOffsetOnAxis(
                ap=pad_rows[:, e:e + 1], axis=0), in_=pad[:, :], in_offset=None).then_inc(sm["pads_written"], 16)
        for e in POOL_SPLITS:
            split_w1(pool, pool, e, "w1_split_pool")

        def step(t):
            i, o = t.back(2), t.back(3)
            if active(i):
                wait(pool, "y_ready", done(o))
                wait(pool, "summed", 16 * o.n)
                wait(pool, "yb_ready", done(i))
                pool.tensor_tensor(y[:, i.s2], yb[:, i.s2], weight[:, i.s4].to_broadcast([P, D]), ALU.mult
                                   ).then_inc(sm["y_ready"], 1)
            if active(o):
                if o.fixed and not active(i):
                    wait(pool, "y_ready", done(o))
                    wait(pool, "summed", 16 * o.n)
                pool.indirect_dma_start(out=dram["sum"], out_offset=bass.IndirectOffsetOnAxis(
                    ap=token[:, o.s4:o.s4 + 1], axis=0), in_=y[:, o.s2], in_offset=None, compute_op=ALU.add
                    ).then_inc(sm["summed"], 16)

        pipeline(pool, step)
        pool.wait_ge(sm["summed"], 16 * TILES)

    @block.tensor
    def _(pe):
        mm = nc.tensor.matmul
        pe.wait_ge(sm["consts_made2"], 2)
        pe.wait_ge(sm["tables_ready"], 2)
        pe.wait_ge(sm["w1_split"], E - len(POOL_SPLITS))
        pe.wait_ge(sm["w1_split_pool"], len(POOL_SPLITS))
        pe.wait_ge(sm["wo_split"], 1)

        def product(out, hi, lo, w_hi, w_lo, chunks, columns, lo_ready):
            for k in range(chunks):
                part = slice(k * P, (k + 1) * P)
                mm(out, hi[:, part], w_hi[:, k, columns], start=k == 0, stop=False)
                mm(out, hi[:, part], w_lo[:, k, columns], start=False, stop=False)
            lo_ready()
            for k in range(chunks):
                last = mm(out, lo[:, k * P:(k + 1) * P], w_hi[:, k, columns], start=False, stop=k == chunks - 1)
            return last

        def load_expert(i):
            return pe.value_load(exp_tab[0:1, bass.ds(i.n, 1)], min_val=0, max_val=E - 1)

        ahead = []

        def step(t):
            i = t.back(1)
            if active(i):
                e = ahead.pop() if ahead else load_expert(i)
            i = t
            if active(i):
                wait(pe, f"xe_loaded{i.s4}", 16 * (i.j + i.r // 4) + 16)
                wait(pe, "xet_split", done(i.back(1)))
                for k in range(DC):
                    last = nc.tensor.transpose(psX[:, k * P:(k + 1) * P], xe[:, i.s4, k * P:(k + 1) * P], ident[:, :])
                last.then_inc(sm["x_transposed"], 1)
            i = t.back(1)
            if active(i):
                wait(pe, "xet_rounded", done(i))
                wait(pe, "hb_ready", done(i.back(2)))
                product(psHb[:, i.s2, :], xet_hi[:, i.s2], xet_lo[:, i.s2], w1_hi, w1_lo, DC, bass.ds(e * H2 + H, H),
                        lambda: wait(pe, "xet_split", done(i))).then_inc(sm["b_product"], 1)
            o = t.back(2)
            if active(o):
                wait(pe, "g_ready", done(o))
                wait(pe, "gt_split", done(o.back(1)))
                for k in range(HC):
                    last = nc.tensor.transpose(psG[:, k * P:(k + 1) * P], g[:, o.s2, k * P:(k + 1) * P], ident[:, :])
                last.then_inc(sm["g_transposed"], 1)
            if active(i):
                wait(pe, "ha_ready", done(i.back(2)))
                product(psHa[:, i.s2, :], xet_hi[:, i.s2], xet_lo[:, i.s2], w1_hi, w1_lo, DC, bass.ds(e * H2, H),
                        lambda: None).then_inc(sm["a_product"], 1)
            if active(i) and active(t) and t.r % 4 != 3:
                ahead.append(load_expert(t))
            if active(o):
                wait(pe, "gt_rounded", done(o))
                wait(pe, "yb_ready", done(o.back(2)))
                product(psY[:, o.s2, 0:D], gt_hi[:, o.s2], gt_lo[:, o.s2], wo_hi, wo_lo, HC, slice(0, D),
                        lambda: wait(pe, "gt_split", done(o))).then_inc(sm["y_product"], 1)

        pipeline(pe, step)

    @block.scalar
    def _(act):
        copy = nc.scalar.copy
        act.wait_ge(sm["wo_loaded"], 16)
        copy(wo_hi[:, :, :], wo_raw[:, :, :]).then_inc(sm["wo_rounded"], 1)
        for e in range(E):
            act.wait_ge(dram["w1_loaded"][e], 16)
            copy(w1_hi[:, :, e * H2:(e + 1) * H2], w1_raw[:, :, e * H2:(e + 1) * H2]).then_inc(sm["w1_rounded"], 1)

        def step(t):
            i = t
            if active(i):
                wait(act, "x_transposed", done(i))
                wait(act, "a_product", done(i.back(2)))
                copy(xet_hi[:, i.s2], psX[:, 0:D]).then_inc(sm["xet_rounded"], 1)
            o = t.back(2)
            if active(o):
                wait(act, "g_transposed", done(o))
                wait(act, "y_product", done(o.back(2)))
                copy(gt_hi[:, o.s2], psG[:, :]).then_inc(sm["gt_rounded"], 1)
            i = t.back(1)
            if active(i):
                wait(act, "hb_ready", done(i))
                wait(act, "g_ready", done(i.back(2)))
                nc.scalar.activation(sig[:, i.s2], hb[:, i.s2], ACT.Sigmoid).then_inc(sm["sig_ready"], 1)

        pipeline(act, step)

    @block.vector
    def _(dve):
        v = nc.vector
        links = 0

        def link(ins):
            nonlocal links
            links += 1
            ins.then_inc(sm["table_link"], 1)
            dve.wait_ge(sm["table_link"], links)

        dve.wait_ge(sm["consts_made2"], 2)
        last = base[:, 0, :]
        link(v.tensor_scalar(pad_place[:, :], last, partition[:, :], None, ALU.add))
        v.tensor_copy(pad_rows[:, :], pad_place[:, :]).then_inc(sm["pad_rows_ready"], 1)
        link(v.tensor_tensor(cnt[:, :], last, listbase[:, :], ALU.subtract))
        link(v.tensor_scalar(cnti[:, :], cnt[:, :], float(P - 1), None, ALU.add))
        link(v.tensor_single_scalar(cnti[:, :], cnti[:, :], 7, ALU.logical_shift_right))
        link(v.tensor_copy(ntile[:, :], cnti[:, :]))
        link(v.tensor_copy(upto[:, 0:1], ntile[:, 0:1]))
        for e in range(1, E):
            link(v.tensor_tensor(upto[:, e:e + 1], upto[:, e - 1:e], ntile[:, e:e + 1], ALU.add))
        link(v.tensor_scalar(skip[:, :], ntile[:, :], -float(P), float(STRIDE), ALU.mult, ALU.add))
        link(v.tensor_scalar(rowf[:, :], number[:, :], float(P), None, ALU.mult))
        link(v.memset(expf[:, :], 0.0))
        for e in range(E):
            link(v.tensor_scalar(past[:, :], number[:, :], upto[:, e:e + 1], None, ALU.is_ge))
            link(v.scalar_tensor_tensor(rowf[:, :], past[:, :], skip[:, e:e + 1], rowf[:, :], ALU.mult, ALU.add))
            link(v.tensor_tensor(expf[:, :], expf[:, :], past[:, :], ALU.add))
        v.tensor_scalar(row_tab[:, :], rowf[:, :], float(E * STRIDE), None, ALU.min).then_inc(sm["tables_ready"], 1)
        v.tensor_scalar(exp_tab[:, :], expf[:, :], float(E - 1), None, ALU.min).then_inc(sm["tables_ready"], 1)
        dve.wait_ge(sm["tables_ready"], 2)
        dve.wait_ge(sm["wo_rounded"], 1)
        v.tensor_tensor(wo_lo[:, :, :], wo_raw[:, :, :], wo_hi[:, :, :].bitcast(F32), ALU.subtract
                        ).then_inc(sm["wo_split"], 1)
        for e in range(E):
            if e not in POOL_SPLITS:
                split_w1(v, dve, e, "w1_split")
        dve.wait_ge(sm["w1_split"], E - len(POOL_SPLITS))
        dve.wait_ge(sm["wo_split"], 1)
        dve.wait_ge(dram["biases_loaded"], 16 * (1 + E))

        def step(t):
            x, i, o = t, t.back(1), t.back(2)
            if active(x):
                wait(dve, "xet_rounded", done(x))
                v.tensor_tensor(xet_lo[:, x.s2], psX[:, 0:D], xet_hi[:, x.s2].bitcast(F32), ALU.subtract
                                ).then_inc(sm["xet_split"], 1)
            if active(i):
                e = dve.value_load(exp_tab[0:1, bass.ds(i.n, 1)], min_val=0, max_val=E - 1)
                wait(dve, f"xe_loaded{i.s4}", 16 * (i.j + i.r // 4) + 16)
                wait(dve, "summed", 16 * (i.n - 3))
                wait(dve, "b_product", done(i))
                wait(dve, "sig_ready", done(i.back(2)))
                v.tensor_tensor(hb[:, i.s2], psHb[:, i.s2, :], b1[:, bass.ds(e * H2 + H, H)], ALU.add
                                ).then_inc(sm["hb_ready"], 1)
                v.tensor_copy(token[:, i.s4:i.s4 + 1], xe[:, i.s4, ROW - 1:ROW])
                v.tensor_copy(weight[:, i.s4], xe[:, i.s4, bass.ds(e + D, 1)]).then_inc(sm["token_ready"], 1)
            if active(o):
                wait(dve, "gt_rounded", done(o))
                v.tensor_tensor(gt_lo[:, o.s2], psG[:, :], gt_hi[:, o.s2].bitcast(F32), ALU.subtract
                                ).then_inc(sm["gt_split"], 1)
            if active(i):
                wait(dve, "a_product", done(i))
                wait(dve, "g_transposed", done(i.back(2)))
                v.tensor_tensor(g[:, i.s2], psHa[:, i.s2, :], b1[:, bass.ds(e * H2, H)], ALU.add
                                ).then_inc(sm["ha_ready"], 1)
                wait(dve, "ha_ready", done(i))
                wait(dve, "sig_ready", done(i))
                v.tensor_tensor(g[:, i.s2], g[:, i.s2], sig[:, i.s2], ALU.mult).then_inc(sm["g_ready"], 1)
            if active(o):
                wait(dve, "y_product", done(o))
                wait(dve, "y_ready", done(o.back(2)))
                v.tensor_tensor(yb[:, o.s2], psY[:, o.s2, 0:D], bo[:, :], ALU.add).then_inc(sm["yb_ready"], 1)

        pipeline(dve, step)


def final_norm(nc, ctx, io, dram):
    T, D = dram["sum"].shape
    T -= P
    QC = 4
    B = T // (P * QC)

    def sb(name, shape, dt=F32):
        return ctx.enter_context(nc.sbuf_tensor(name, shape, dt))

    total = sb("total", [P, 4, QC, D])
    stats = sb("stats3", [P, 4, QC, 6])
    mv = sb("mv3", [P, 4, QC, 2])
    vare = sb("vare3", [P, 4, QC])
    rstd = sb("rstd3", [P, 4, QC])
    nmean = sb("nmean3", [P, 4, QC])
    shift = sb("shift3", [P, 4, QC])
    neg_one = sb("neg_one3", [P, QC])
    eps_c = sb("eps3", [P, QC])
    neg_half = sb("neg_half3", [P, QC])
    result = sb("result", [P, 4, QC, D])
    names = ["consts_made3", "stats3_ready", "var3_ready", "rstd3_ready", "normed"]
    names += [f"total_loaded{s}" for s in range(4)] + [f"result_stored{s}" for s in range(4)]
    sm = {n: ctx.enter_context(nc.semaphore(n)) for n in names}

    def wait(eng, name, value):
        if isinstance(value, int) and value <= 0:
            return
        eng.wait_ge(sm[name], value)

    def active(b):
        return not b.fixed or 0 <= b.n < B

    def pipeline(eng, step):
        for r in range(8):
            step(Step(0, r))
        with eng.Fori(2, B // 4) as j:
            for r in range(4):
                step(Step(j, r))
        for r in range(3):
            step(Step(B // 4, r))

    block = ctx.enter_context(nc.Block())
    rows = dram["sum"][0:T, :].rearrange("(b p c) d -> b p c d", p=P, c=QC)
    out = dram["out"].rearrange("b s d -> (b s) d").rearrange("(b p c) d -> b p c d", p=P, c=QC)

    @block.sync
    def _(sp):
        def step(t):
            if active(t):
                wait(sp, "normed", t.n - 3)
                sp.dma_start(total[:, t.s4], rows[bass.ds(t.n, 1)].rearrange("o p c d -> (o p) c d")
                             ).then_inc(sm[f"total_loaded{t.s4}"], 16)

        pipeline(sp, step)

    @block.scalar
    def _(act):
        def step(t):
            b = t.back(3)
            if active(b):
                wait(act, "rstd3_ready", 3 * b.n + 3)
                wait(act, f"result_stored{b.s4}", 16 * (b.j + b.r // 4))
                for c in range(QC):
                    last = nc.scalar.activation(result[:, b.s4, c, :], total[:, b.s4, c, :], ACT.Identity,
                                                scale=rstd[:, b.s4, c:c + 1], bias=shift[:, b.s4, c:c + 1])
                last.then_inc(sm["normed"], 1)
                wait(act, "normed", b.n + 1)
                act.dma_start(out[bass.ds(b.n, 1)].rearrange("o p c d -> (o p) c d"), result[:, b.s4]
                              ).then_inc(sm[f"result_stored{b.s4}"], 16)

        pipeline(act, step)
        for s in range(4):
            act.wait_ge(sm[f"result_stored{s}"], 16 * (B // 4))

    @block.gpsimd
    def _(pool):
        pool.memset(eps_c[:, :], EPS)
        pool.memset(neg_one[:, :], -1.0)
        pool.memset(neg_half[:, :], -0.5).then_inc(sm["consts_made3"], 1)
        pool.wait_ge(sm["consts_made3"], 1)

        def step(t):
            b = t.back(2)
            if active(b):
                wait(pool, "var3_ready", b.n + 1)
                pool.tensor_tensor(vare[:, b.s4], mv[:, b.s4, :, 1], eps_c[:, :], ALU.add)
                pool.tensor_tensor(nmean[:, b.s4], mv[:, b.s4, :, 0], neg_one[:, :], ALU.mult
                                   ).then_inc(sm["rstd3_ready"], 1)
                wait(pool, "rstd3_ready", 3 * b.n + 1)
                pool.tensor_tensor(rstd[:, b.s4], vare[:, b.s4], neg_half[:, :], ALU.pow).then_inc(sm["rstd3_ready"], 1)
                wait(pool, "rstd3_ready", 3 * b.n + 2)
                pool.tensor_tensor(shift[:, b.s4], nmean[:, b.s4], rstd[:, b.s4], ALU.mult
                                   ).then_inc(sm["rstd3_ready"], 1)

        pipeline(pool, step)

    @block.vector
    def _(dve):
        v = nc.vector

        def step(t):
            b = t.back(1)
            if active(b):
                wait(dve, "stats3_ready", b.n + 1)
            if active(t):
                wait(dve, f"total_loaded{t.s4}", 16 * (t.j + t.r // 4) + 16)
                for c in range(QC):
                    last = v.bn_stats(stats[:, t.s4, c, :], total[:, t.s4, c, :])
                last.then_inc(sm["stats3_ready"], 1)
            if active(b):
                for c in range(QC):
                    last = v.bn_aggr(mv[:, b.s4, c, :], stats[:, b.s4, c, :])
                last.then_inc(sm["var3_ready"], 1)

        pipeline(dve, step)


def decoder_layer(nc, io, out):
    B, S, D = io["x"].shape
    E = io["wg_t"].shape[1]
    H2 = io["f1_b"].shape[1]
    T = B * S
    stride = T + P
    with ExitStack() as ctx:
        dram = {
            "q": nc.dram_tensor("q_parts", (2, 3, D, S), BF16, kind="Internal").ap(),
            "sum": nc.dram_tensor("sums", (T + P, D), F32, kind="Internal").ap(),
            "lists": nc.dram_tensor("lists", (E * stride + P, D + E + 1), F32, kind="Internal").ap(),
            "base": ctx.enter_context(nc.sbuf_tensor("base", [P, 2, E], F32)),
            "b1": ctx.enter_context(nc.sbuf_tensor("f_b1", [P, E * H2], F32)),
            "bo": ctx.enter_context(nc.sbuf_tensor("f_bo", [P, D], F32)),
            "biases_loaded": ctx.enter_context(nc.semaphore("biases_loaded")),
            "w1_loaded": [ctx.enter_context(nc.semaphore(f"w1_loaded{e}")) for e in range(E)],
            "stride": stride,
            "out": out,
        }
        with nc.sbuf_tensor("w1_raw", [P, D // P, E * H2], F32) as w1_raw:
            dram["w1_raw"] = w1_raw
        for phase in (attention, experts, final_norm):
            with ExitStack() as own:
                phase(nc, own, io, dram)


def kernel(**inputs):
    from concourse import bacc
    from concourse.bass_utils import run_bass_kernel_spmd

    a = {k: np.asarray(v) for k, v in inputs.items()}
    D = a["x"].shape[2]
    laid = {
        "x": a["x"],
        "x_t": a["x"].transpose(0, 2, 1),
        "context": a["ctx_1024"],
        "context_t": a["ctx_1024"].reshape(-1, D).T,
        "mask": a["fside_1xSxS2_0"][0],
        "wq_t": a["L0_attn_Wq"].T,
        "wk_t": a["L0_attn_Wk"].T,
        "wv_t": a["L0_attn_Wv"].T,
        "w1": a["L0_xattn_W1"],
        "w2_t": a["L0_xattn_W2"].T,
        "b1": a["L0_xattn_b1"].reshape(-1, P).T,
        "b2": a["L0_xattn_b2"].reshape(-1, P).T,
        "wg_t": a["L0_ffn_Wg"].T,
        "f1_t": a["L0_ffn_W1"].transpose(0, 2, 1),
        "f1_b": a["L0_ffn_b1"],
        "wo_t": a["L0_ffn_Wo"].T,
        "bo": a["L0_ffn_bo"],
    }
    nc = bacc.Bacc("TRN2", target_bir_lowering=False, num_devices=1)
    arrays, io = {}, {}
    for name, array in laid.items():
        array = np.ascontiguousarray(array)
        arrays[f"in_{name}"] = array
        io[name] = nc.dram_tensor(f"in_{name}", array.shape, mybir.dt.from_np(array.dtype), kind="ExternalInput").ap()
    out = nc.dram_tensor("out", a["x"].shape, F32, kind="ExternalOutput").ap()
    decoder_layer(nc, io, out)
    result = run_bass_kernel_spmd(nc, [arrays], core_ids=[0])
    return result.results[0]["out"]
```
